# Optimizing a Trainium2 kernel written in Bass

```python
import numpy as np
import jax
import jax.numpy as jnp

def _softmax(x, axis=-1):
    return jax.nn.softmax(x, axis=axis)

def _gelu(x):
    return jax.nn.gelu(x, approximate=True)

def _silu(x):
    return jax.nn.silu(x)

def _sigmoid(x):
    return jax.nn.sigmoid(x)

def _layernorm(x, axis=-1, eps=1e-05):
    m = jnp.mean(x, axis=axis, keepdims=True)
    v = jnp.var(x, axis=axis, keepdims=True)
    return (x - m) / jnp.sqrt(v + eps)

def _scatter_add(tgt, idx, src, axis=0):
    return tgt.at[idx].add(src)

def _segment_sum(src, seg, n):
    return jax.ops.segment_sum(src, seg, n)
kernel_name = 'mk_macaron_d2_jaxref_r8_421d48'

def setup_inputs(seed: int=0):
    np.random.seed(seed)
    _w = jnp.asarray

    def _L0_attn_setup():
        import jax, jax.numpy as jnp
        import numpy as np
        HID = 256
        HEADS = 16
        HD = HID // HEADS
        EPS = 1e-06

        def _heads(x, b, s):
            return x.reshape(b, s, HEADS, HD).transpose(0, 2, 1, 3)
        key = jax.random.key(seed)
        ks = jax.random.split(key, 9)
        s = 1.0 / np.sqrt(HID)
        return {'hidden_states': jax.random.normal(ks[0], (4, 512, HID), jnp.float32), 'q_w': jax.random.normal(ks[1], (HID, HID), jnp.float32) * s, 'q_b': jnp.zeros((HID,), jnp.float32), 'k_w': jax.random.normal(ks[2], (HID, HID), jnp.float32) * s, 'k_b': jnp.zeros((HID,), jnp.float32), 'v_w': jax.random.normal(ks[3], (HID, HID), jnp.float32) * s, 'v_b': jnp.zeros((HID,), jnp.float32), 'o_w': jax.random.normal(ks[4], (HID, HID), jnp.float32) * s, 'o_b': jnp.zeros((HID,), jnp.float32)}
    _L0_attn_in = _L0_attn_setup()

    def _L0_ffn_setup():
        import jax, jax.numpy as jnp
        import numpy as np
        TOP_K = 4
        key = jax.random.key(seed)
        ks = jax.random.split(key, 5)
        H, I, E = (256, 96, 32)
        s = 0.02
        return {'hidden_states': jax.random.normal(ks[0], (1, 128, H), jnp.float32), 'router_w': jax.random.normal(ks[1], (E, H), jnp.float32) * s, 'gate_w': jax.random.normal(ks[2], (E, I, H), jnp.float32) * s, 'up_w': jax.random.normal(ks[3], (E, I, H), jnp.float32) * s, 'down_w': jax.random.normal(ks[4], (E, H, I), jnp.float32) * s}
    _L0_ffn_in = _L0_ffn_setup()

    def _L1_attn_setup():
        import jax, jax.numpy as jnp
        import numpy as np
        T, B, H, N2 = (512, 2, 256, 8)

        def _s4d_kernel(log_dt, A_real_log, A_imag, C_re, C_im, L):
            dt = jnp.exp(log_dt)[:, None]
            A = -jnp.exp(A_real_log) + 1j * A_imag
            dtA = A * dt
            C = (C_re + 1j * C_im) * (jnp.exp(dtA) - 1.0) / A
            vander = jnp.exp(dtA[:, :, None] * jnp.arange(L))
            return 2.0 * jnp.einsum('hn,hnl->hl', C, vander).real
        key = jax.random.key(seed)
        k1, k2, k3, k4, k5 = jax.random.split(key, 5)
        x = jax.random.normal(k1, (T, B, H), dtype=jnp.float32)
        D_param = jax.random.normal(k2, (H,), dtype=jnp.float32)
        u = jax.random.uniform(k3, (H,), dtype=jnp.float32)
        log_dt = u * (jnp.log(0.1) - jnp.log(0.001)) + jnp.log(0.001)
        A_real_log = jnp.full((H, N2), jnp.log(0.5), dtype=jnp.float32)
        A_imag = jnp.broadcast_to(np.pi * jnp.arange(N2, dtype=jnp.float32), (H, N2))
        C_re = jax.random.normal(k4, (H, N2), dtype=jnp.float32)
        C_im = jax.random.normal(k5, (H, N2), dtype=jnp.float32)
        return {'x': x, 'D_param': D_param, 'log_dt': log_dt, 'A_real_log': A_real_log, 'A_imag': A_imag, 'C_re': C_re, 'C_im': C_im}
    _L1_attn_in = _L1_attn_setup()

    def _L1_ffn_setup():
        import jax, jax.numpy as jnp
        import numpy as np
        HIDDEN = 256
        N_EXPERTS = 8
        N_SHARED = 2
        TOP_K = 2
        MOE_FF = 176
        SHARED_FF = N_SHARED * MOE_FF
        SCALE = 2.5
        BATCH, SEQ = (2, 128)
        key = jax.random.key(seed)
        ks = jax.random.split(key, 8)
        s = 0.02
        return {'hidden_states': jax.random.normal(ks[0], (BATCH, SEQ, HIDDEN), jnp.float32), 'gate_w': jax.random.normal(ks[1], (N_EXPERTS, HIDDEN), jnp.float32) * s, 'shared_wg': jax.random.normal(ks[2], (SHARED_FF, HIDDEN), jnp.float32) * s, 'shared_wu': jax.random.normal(ks[3], (SHARED_FF, HIDDEN), jnp.float32) * s, 'shared_wd': jax.random.normal(ks[4], (HIDDEN, SHARED_FF), jnp.float32) * s, 'exp_wg': jax.random.normal(ks[5], (N_EXPERTS, MOE_FF, HIDDEN), jnp.float32) * s, 'exp_wu': jax.random.normal(ks[6], (N_EXPERTS, MOE_FF, HIDDEN), jnp.float32) * s, 'exp_wd': jax.random.normal(ks[7], (N_EXPERTS, HIDDEN, MOE_FF), jnp.float32) * s}
    _L1_ffn_in = _L1_ffn_setup()
    _d = {'L0_attn_hidden_states': _L0_attn_in['hidden_states'], 'L0_attn_q_w': _L0_attn_in['q_w'], 'L0_attn_q_b': _L0_attn_in['q_b'], 'L0_attn_k_w': _L0_attn_in['k_w'], 'L0_attn_k_b': _L0_attn_in['k_b'], 'L0_attn_v_w': _L0_attn_in['v_w'], 'L0_attn_v_b': _L0_attn_in['v_b'], 'L0_attn_o_w': _L0_attn_in['o_w'], 'L0_attn_o_b': _L0_attn_in['o_b'], 'L0_ffn_router_w': _L0_ffn_in['router_w'], 'L0_ffn_gate_w': _L0_ffn_in['gate_w'], 'L0_ffn_up_w': _L0_ffn_in['up_w'], 'L0_ffn_down_w': _L0_ffn_in['down_w'], 'L1_attn_D_param': _L1_attn_in['D_param'], 'L1_attn_log_dt': _L1_attn_in['log_dt'], 'L1_attn_A_real_log': _L1_attn_in['A_real_log'], 'L1_attn_A_imag': _L1_attn_in['A_imag'], 'L1_attn_C_re': _L1_attn_in['C_re'], 'L1_attn_C_im': _L1_attn_in['C_im'], 'L1_ffn_gate_w': _L1_ffn_in['gate_w'], 'L1_ffn_shared_wg': _L1_ffn_in['shared_wg'], 'L1_ffn_shared_wu': _L1_ffn_in['shared_wu'], 'L1_ffn_shared_wd': _L1_ffn_in['shared_wd'], 'L1_ffn_exp_wg': _L1_ffn_in['exp_wg'], 'L1_ffn_exp_wu': _L1_ffn_in['exp_wu'], 'L1_ffn_exp_wd': _L1_ffn_in['exp_wd']}
    _x0 = _d['L0_attn_hidden_states']
    _d['L0_attn_hidden_states'] = jax.random.normal(jax.random.fold_in(jax.random.key(seed), 1), (4, 512, 256), dtype=_x0.dtype)
    del _x0
    return _d

def reference(L0_attn_hidden_states, L0_attn_q_w, L0_attn_q_b, L0_attn_k_w, L0_attn_k_b, L0_attn_v_w, L0_attn_v_b, L0_attn_o_w, L0_attn_o_b, L0_ffn_router_w, L0_ffn_gate_w, L0_ffn_up_w, L0_ffn_down_w, L1_attn_D_param, L1_attn_log_dt, L1_attn_A_real_log, L1_attn_A_imag, L1_attn_C_re, L1_attn_C_im, L1_ffn_gate_w, L1_ffn_shared_wg, L1_ffn_shared_wu, L1_ffn_shared_wd, L1_ffn_exp_wg, L1_ffn_exp_wu, L1_ffn_exp_wd):

    def _L0_attn_ref(hidden_states, q_w, q_b, k_w, k_b, v_w, v_b, o_w, o_b):
        import jax, jax.numpy as jnp
        import numpy as np
        HID = 256
        HEADS = 16
        HD = HID // HEADS
        EPS = 1e-06

        def _heads(x, b, s):
            return x.reshape(b, s, HEADS, HD).transpose(0, 2, 1, 3)
        b, s, _ = hidden_states.shape
        q = _heads(hidden_states @ q_w.T + q_b, b, s)
        k = _heads(hidden_states @ k_w.T + k_b, b, s)
        v = _heads(hidden_states @ v_w.T + v_b, b, s)
        qp = jax.nn.elu(q) + 1.0
        kp = jax.nn.elu(k) + 1.0
        kv = jnp.einsum('bhsd,bhse->bhde', kp, v)
        z = jnp.einsum('bhsd,bhd->bhs', qp, kp.sum(axis=2))[..., None]
        attn = jnp.einsum('bhsd,bhde->bhse', qp, kv) / (z + EPS)
        out = attn.transpose(0, 2, 1, 3).reshape(b, s, HID)
        return out @ o_w.T + o_b

    def _L0_ffn_ref(hidden_states, router_w, gate_w, up_w, down_w):
        import jax, jax.numpy as jnp
        import numpy as np
        TOP_K = 4
        B, S, H = hidden_states.shape
        E = router_w.shape[0]
        x = hidden_states.reshape(-1, H)
        logits = x @ router_w.T
        probs = jax.nn.softmax(logits.astype(jnp.float32), axis=-1)
        rw, sel = jax.lax.top_k(probs, TOP_K)
        rw = rw / jnp.sum(rw, axis=-1, keepdims=True)
        rw = rw.astype(x.dtype)

        def body(acc, expert):
            gw, uw, dw, e = expert
            w_tok = jnp.sum(jnp.where(sel == e, rw, 0.0), axis=-1)
            h = jax.nn.silu(x @ gw.T) * (x @ uw.T)
            y = h @ dw.T
            return (acc + w_tok[:, None] * y, None)
        acc0 = jnp.zeros_like(x)
        out, _ = jax.lax.scan(body, acc0, (gate_w, up_w, down_w, jnp.arange(E)))
        return out.reshape(B, S, H)

    def _L1_attn_ref(x, D_param, log_dt, A_real_log, A_imag, C_re, C_im):
        import jax, jax.numpy as jnp
        import numpy as np
        T, B, H, N2 = (512, 2, 256, 8)

        def _s4d_kernel(log_dt, A_real_log, A_imag, C_re, C_im, L):
            dt = jnp.exp(log_dt)[:, None]
            A = -jnp.exp(A_real_log) + 1j * A_imag
            dtA = A * dt
            C = (C_re + 1j * C_im) * (jnp.exp(dtA) - 1.0) / A
            vander = jnp.exp(dtA[:, :, None] * jnp.arange(L))
            return 2.0 * jnp.einsum('hn,hnl->hl', C, vander).real
        seq_len = x.shape[0]
        residual = x * D_param
        xb = jnp.transpose(x, (1, 2, 0))
        k = _s4d_kernel(log_dt, A_real_log, A_imag, C_re, C_im, seq_len)
        n = 2 * seq_len
        k_f = jnp.fft.rfft(k, n=n)
        x_f = jnp.fft.rfft(xb, n=n)
        out = jnp.fft.irfft(x_f * k_f, n=n)[..., :seq_len]
        return jnp.transpose(out, (2, 0, 1)) + residual

    def _L1_ffn_ref(hidden_states, gate_w, shared_wg, shared_wu, shared_wd, exp_wg, exp_wu, exp_wd):
        import jax, jax.numpy as jnp
        import numpy as np
        HIDDEN = 256
        N_EXPERTS = 8
        N_SHARED = 2
        TOP_K = 2
        MOE_FF = 176
        SHARED_FF = N_SHARED * MOE_FF
        SCALE = 2.5
        BATCH, SEQ = (2, 128)
        B, S, D = hidden_states.shape
        T = B * S
        xf = hidden_states.reshape(T, D)
        scores = jax.nn.sigmoid(xf @ gate_w.T)
        topk_w, topk_idx = jax.lax.top_k(scores, TOP_K)
        topk_w = topk_w / (topk_w.sum(axis=-1, keepdims=True) + 1e-20)
        topk_w = topk_w * SCALE
        shared_out = jax.nn.silu(xf @ shared_wg.T) * (xf @ shared_wu.T) @ shared_wd.T
        h = jax.nn.silu(jnp.einsum('td,efd->etf', xf, exp_wg)) * jnp.einsum('td,efd->etf', xf, exp_wu)
        all_out = jnp.einsum('etf,edf->etd', h, exp_wd)
        picked = all_out[topk_idx, jnp.arange(T)[:, None]]
        routed_out = (topk_w[..., None] * picked).sum(axis=1)
        return (shared_out + routed_out).reshape(B, S, D)
    x = L0_attn_hidden_states
    x = x + 0.5 * _L0_ffn_ref(_layernorm(x, axis=-1), L0_ffn_router_w, L0_ffn_gate_w, L0_ffn_up_w, L0_ffn_down_w)
    x = x + _L0_attn_ref(_layernorm(x, axis=-1), L0_attn_q_w, L0_attn_q_b, L0_attn_k_w, L0_attn_k_b, L0_attn_v_w, L0_attn_v_b, L0_attn_o_w, L0_attn_o_b)
    x = x + 0.5 * _L0_ffn_ref(_layernorm(x, axis=-1), L0_ffn_router_w, L0_ffn_gate_w, L0_ffn_up_w, L0_ffn_down_w)
    x = x + 0.5 * _L1_ffn_ref(_layernorm(x, axis=-1), L1_ffn_gate_w, L1_ffn_shared_wg, L1_ffn_shared_wu, L1_ffn_shared_wd, L1_ffn_exp_wg, L1_ffn_exp_wu, L1_ffn_exp_wd)
    x = x + _L1_attn_ref(_layernorm(x, axis=-1), L1_attn_D_param, L1_attn_log_dt, L1_attn_A_real_log, L1_attn_A_imag, L1_attn_C_re, L1_attn_C_im)
    x = x + 0.5 * _L1_ffn_ref(_layernorm(x, axis=-1), L1_ffn_gate_w, L1_ffn_shared_wg, L1_ffn_shared_wu, L1_ffn_shared_wd, L1_ffn_exp_wg, L1_ffn_exp_wu, L1_ffn_exp_wd)
    return x

_drawn_inputs = setup_inputs


def setup_inputs(seed=0):
    import zlib

    import numpy as np

    out = dict(_drawn_inputs(seed))
    spreads = {'L0_attn_q_b': (0.0, 2.0),
     'L0_attn_k_b': (0.0, 2.0),
     'L0_attn_v_b': (0.0, 0.1),
     'L0_attn_o_b': (0.0, 0.1),
     'L1_attn_A_real_log': (-0.6931471824645996, 0.6)}
    factors = {'L0_attn_q_w': 6.655,
     'L0_attn_k_w': 3.413,
     'L0_ffn_router_w': 8.0,
     'L0_ffn_gate_w': 8.0,
     'L0_ffn_up_w': 8.0,
     'L0_ffn_down_w': 8.0,
     'L1_ffn_gate_w': 4.052,
     'L1_ffn_shared_wg': 4.177,
     'L1_ffn_shared_wu': 4.13,
     'L1_ffn_shared_wd': 4.118,
     'L1_ffn_exp_wg': 3.515,
     'L1_ffn_exp_wu': 3.486,
     'L1_ffn_exp_wd': 3.463}
    for name, (base, spread) in spreads.items():
        noise = np.random.default_rng([zlib.crc32(name.encode()), seed]).standard_normal(out[name].shape)
        drawn = base * np.exp(spread * noise) if base else spread * noise
        out[name] = jnp.asarray(drawn.astype(out[name].dtype))
    for name, factor in factors.items():
        out[name] = (out[name] * factor).astype(out[name].dtype)
    return out
```

```python
from contextlib import ExitStack
from collections import namedtuple

import numpy as np
import concourse.bass as bass
from concourse import mybir

F32 = mybir.dt.float32
F16 = mybir.dt.float16
ALU = mybir.AluOpType
ACT = mybir.ActivationFunctionType
AXX = mybir.AxisListType.X

P = 128
HID = 256
HC = HID // P
NBLK = 4
BLK = 512
TPB = BLK // P
E0, I0, TOP0 = 32, 96, 4
E1, I1, TOP1, SHARED1 = 8, 176, 2, 352
C0 = E0 * I0 // P
C1 = -(-(E1 * I1 + SHARED1) // P)
R1 = E1 + SHARED1 // I1
WCOLS = HC * P + HC * P + HID
QCHUNKS = 2
LATE = C1 + QCHUNKS
HEADS, HD = 16, 16
NS4 = 8
EPS = 1e-5
ATT_EPS = 1e-6

XS = 16.0
WS = 64.0
RS = 256.0
HS = 4.0
XW = 1.0 / (XS * WS)
P_SCALE = HS / (XS * WS * RS)
HALF = 0.5
ROUTE1_SCALE = 2.5
NEVER = -1e30
TAKEN = -3e38
SENT0, SENT1 = 8 - TOP0, 8 - TOP1
LO_ROW = 32

PQB, PDT, PD = 0, 2, 4
PAR, PAI, PCR, PCI = 6, 22, 38, 54
PR0 = 70
PR1 = PR0 + HC * E0
PCOLS = PR1 + HC * E1

Ffn = namedtuple("Ffn", "phase chunks k0 r0 kind late")


def build(nc, x_in, w0_in, late_in, small_in, kvb_in, ob_in, ow_in, sel_in, ident_in, mask_in, out):
    ctx = ExitStack()
    with ctx:
        def sb(name, shape, dt):
            return ctx.enter_context(nc.sbuf_tensor(name, shape, dt))

        def pb(name, shape, dt):
            return ctx.enter_context(nc.psum_tensor(name, shape, dt))

        def sem(name):
            return ctx.enter_context(nc.semaphore(name))

        x = sb("x", [P, NBLK * TPB, HID], F32)
        w0_hi = sb("w0_hi", [P, C0, WCOLS], F16)
        w0_lo = sb("w0_lo", [P, C0, WCOLS], F16)
        w1_hi = sb("w1_hi", [P, LATE, WCOLS], F16)
        w1_lo = sb("w1_lo", [P, LATE, WCOLS], F16)
        sel = sb("sel", [P, (C0 + C1) * P], F16)
        xT_hi = sb("xT_hi", [P, HC, NBLK, BLK], F16)
        xT_lo = sb("xT_lo", [P, HC, NBLK, BLK], F16)
        xn = sb("xn", [P, 2, HID], F32)
        wT = sb("wT", [P, 2, BLK], F16)
        ws = [sb("ws0", [P, TPB, P], F16), sb("ws1", [P, TPB, P], F16)]
        diag_hi = sb("diag_hi", [P, NBLK, HC, P], F16)
        diag_lo = sb("diag_lo", [P, NBLK, HC, P], F16)
        o_w = sb("o_w", [P, HC, HID], F32)
        ident = sb("ident", [P, P], F32)
        ident16 = sb("ident16", [P, P], F16)
        mask = sb("mask", [P, P], F32)
        kv_m = sb("kv_m", [P, 2, P], F32)
        ks_m = sb("ks_m", [P, 2, P], F32)
        small = sb("small", [P, PCOLS], F32)
        rt_hi = sb("rt_hi", [P, PCOLS - PR0], F16)
        rt_lo = sb("rt_lo", [P, PCOLS - PR0], F16)
        bn = sb("bn", [P, TPB, 6], F32)
        mv = sb("mv", [P, TPB, 2], F32)
        ve = sb("ve", [P, TPB], F32)
        mhalf = sb("mhalf", [P, TPB], F32)
        rstd = sb("rstd", [P, TPB], F32)
        lb = [sb("lb0", [P, TPB, E0 + SENT0], F32), sb("lb1", [P, TPB, E1 + SENT1], F32)]
        rb = [sb("rb0", [P, TPB, E0 + SENT0], F32), sb("rb1", [P, TPB, E1 + SENT1], F32)]
        m8 = sb("m8", [P, TPB, 8], F32)
        top = [sb("top0", [P, TPB, 8], F32), sb("top1", [P, TPB, 8], F32)]
        ex = sb("ex", [P, TPB, E0], F32)
        wf = sb("wf", [P, TPB, E0], F32)
        rsum = sb("rsum", [P, TPB], F32)
        rrec = sb("rrec", [P, TPB], F32)

        WORK = 5896
        work = sb("work", [P, WORK], F32)
        silu = work[:, 0:1024].rearrange("p (a n) -> p a n", a=2)
        pbuf = work[:, 1024:1536]
        qbuf = work[:, 1536:2560].rearrange("p (a n) -> p a n", a=2)
        h_hi = work[:, 2560:3072].bitcast(F16).rearrange("p (a n) -> p a n", a=2)
        h_lo = work[:, 3072:3584].bitcast(F16).rearrange("p (a n) -> p a n", a=2)
        NSTAGE = 3
        stage = work[:, 3584:3584 + NSTAGE * WCOLS].rearrange("p (a n) -> p a n", a=NSTAGE)
        k_raw = work[:, 0:1024].rearrange("p (t n) -> p t n", t=TPB)
        attn = work[:, 0:1024].rearrange("p (g n) -> p g n", g=2)
        k_pos = work[:, 1024:2048].rearrange("p (t n) -> p t n", t=TPB)
        VW = 2 * (P + 1)
        v_sb = work[:, 2048:2048 + TPB * VW].rearrange("p (t n) -> p t n", t=TPB)
        QO = 2048 + TPB * VW
        q_raw = work[:, QO:QO + 1024].rearrange("p (m n) -> p m n", m=2)
        den = work[:, QO:QO + 512]
        q_pos = work[:, QO + 1024:QO + 2048].rearrange("p (m n) -> p m n", m=2)
        KVB = QO + 2048
        kv_b = work[:, KVB:KVB + 512]
        o_b = work[:, KVB + 512:KVB + 768]
        assert KVB + 768 <= WORK and 3584 + NSTAGE * WCOLS <= WORK

        gate_ps = [pb("gate_ps0", [P, 512], F32), pb("gate_ps1", [P, 512], F32)]
        up_ps = [pb("up_ps0", [P, 512], F32), pb("up_ps1", [P, 512], F32)]
        wb_ps = pb("wb_ps", [P, 512], F32)
        y_ps = [pb("y_ps0", [P, 512], F32), pb("y_ps1", [P, 512], F32)]
        misc = pb("misc", [P, 512], F32)
        misc16 = misc[:, :].bitcast(F16)

        def y_tile(t):
            return y_ps[t // 2][:, (t % 2) * HID:(t % 2 + 1) * HID]

        ld_const = sem("ld_const")
        ld_x0 = sem("ld_x0")
        ld_x = sem("ld_x")
        ld_att = sem("ld_att")
        ld_w = [sem(f"ld_w{i}") for i in range(NSTAGE)]
        w_hi_done = sem("w_hi_done")
        w_lo_done = sem("w_lo_done")
        ready = sem("ready")
        par_act = sem("par_act")
        par_dve = sem("par_dve")
        stats = sem("stats")
        rstd_done = sem("rstd_done")
        xn_done = sem("xn_done")
        xT_ps = sem("xT_ps")
        xT_hi_done = sem("xT_hi_done")
        xT_lo_done = sem("xT_lo_done")
        logits_ps = sem("logits_ps")
        route_dve = [sem("route0_dve"), sem("route1_dve")]
        shifted = sem("shifted")
        expd = sem("expd")
        ws_done = sem("ws_done")
        wT_ps = sem("wT_ps")
        wT_done = sem("wT_done")
        gate_done = sem("gate_done")
        up_done = sem("up_done")
        wb_done = sem("wb_done")
        silu_done = sem("silu_done")
        p_done = sem("p_done")
        q_done = sem("q_done")
        h_hi_done = sem("h_hi_done")
        h_lo_done = sem("h_lo_done")
        down_done = sem("down_done")
        x_done = sem("x_done")
        y_tmp = sem("y_tmp")
        kv_ps_done = sem("kv_ps_done")
        k_raw_done = sem("k_raw_done")
        q_ps_done = sem("q_ps_done")
        q_raw_done = sem("q_raw_done")
        elu_min = sem("elu_min")
        elu_exp = sem("elu_exp")
        elu_done = sem("elu_done")
        sums_ps = sem("sums_ps")
        sums_done = sem("sums_done")
        ratio_ps = sem("ratio_ps")
        ratio_dve = sem("ratio_dve")
        attn_done = sem("attn_done")
        o_ps_done = sem("o_ps_done")
        s4_ps_done = sem("s4_ps_done")
        w_ready = sem("w_ready")
        y_add = sem("y_add")
        dve_init = sem("dve_init")
        waited = sem("waited")
        stored = sem("stored")

        block = ctx.enter_context(nc.Block())

        FFNS = [Ffn(0, C0, 0, 0, 0, True), Ffn(2, C0, 4 * C0, 4, 0, False),
                Ffn(3, C1, 8 * C0, 8, 1, False), Ffn(5, C1, 8 * C0 + 4 * C1, 12, 1, False)]
        ATT_PHASE, S4_PHASE = 1, 4
        SHAPE = {0: (4, 1, 3), 1: (2, 2, 2)}
        TCH, RCH = 4, 2
        for kind, chunks in ((0, C0), (1, C1)):
            ti, tp, ri = SHAPE[kind]
            assert ti * tp == TPB and 1 + ti * TCH + ri * RCH + 1 == chunks
        W_HI, W_LO = (w0_hi, w1_hi), (w0_lo, w1_lo)
        NEXP, NTOP = (E0, E1), (TOP0, TOP1)
        SEL0 = (0, C0 * P)
        RT0 = (0, HC * E0)

        def nxt(b):
            return (b + 1) % NBLK if isinstance(b, int) else (b + 1) & (NBLK - 1)

        def odd(b):
            return b % 2 if isinstance(b, int) else b & 1

        def at(b):
            return b if isinstance(b, int) or b.max_val < NBLK else b & (NBLK - 1)

        def one(ap_index):
            return bass.ds(ap_index, 1)

        S = {}
        s_at = [0]

        def s4_array(name, n=16):
            S[name] = work[:, s_at[0]:s_at[0] + n]
            s_at[0] += n

        for nm in ("dt", "kc0", "kc1", "kc2", "kc3"):
            s4_array(nm, HC)
        for nm in ("are", "a", "ang0", "turn", "ang", "th", "sin", "sh", "em1", "ea", "cm1", "cos", "wre", "wim",
                   "ere", "t1", "t2", "inv", "fre", "fim", "cre", "cim", "nre", "nim", "aren", "omt"):
            s4_array(nm)
        assert s_at[0] <= 1024
        PAR_A, PAR_T = 2, 9

        def pe_split3(pe, outs, lhs_hi, lhs_lo, rhs_hi, rhs_lo, start, stop, group=True):
            steps = ((lhs_hi, rhs_hi), (lhs_hi, rhs_lo), (lhs_lo, rhs_hi))
            for n, (a, c) in enumerate(steps):
                last = pe.matmul(outs, a, c, start=start and n == 0, stop=stop and n == 2,
                                 skip_group_check=not group)
            return last

        def pe_inner(pe, outs, f, b, c, col):
            hi, lo = W_HI[f.kind], W_LO[f.kind]
            for hc in range(HC):
                a = col + hc * P
                last = pe_split3(pe, outs, hi[:, one(c), a:a + P], lo[:, one(c), a:a + P],
                                 xT_hi[:, hc, one(at(b)), :], xT_lo[:, hc, one(at(b)), :],
                                 hc == 0, hc == HC - 1)
            return last

        def pe_gate_up(pe, f, b, c, par):
            k = f.k0 + b * f.chunks + c
            pe.wait_ge(silu_done, k + 1)
            pe_inner(pe, gate_ps[par][:, :], f, b, c, 0).then_inc(gate_done, 1)
            pe.wait_ge(p_done, k + 1)
            pe_inner(pe, up_ps[par][:, :], f, b, c, HC * P).then_inc(up_done, 1)

        def pe_spread(pe, f, b, c):
            k = f.k0 + b * f.chunks + c
            pe.wait_ge(q_done, k + 2)
            pe.matmul(wb_ps[:, :], sel[:, bass.ds(c * P + SEL0[f.kind], P)], wT[:, one(odd(b)), :],
                      start=True, stop=True).then_inc(wb_done, 1)

        def pe_down(pe, f, b, c, par, first=False, final=False):
            k = f.k0 + b * f.chunks + c
            hi, lo = W_HI[f.kind], W_LO[f.kind]
            w = 2 * HC * P
            if first:
                pe.wait_ge(x_done, 4 * f.phase + b + 4)
            pe.wait_ge(h_lo_done, k + 3)
            for t in range(TPB):
                last = pe_split3(pe, y_tile(t), h_hi[:, par, t * P:(t + 1) * P],
                                 h_lo[:, par, t * P:(t + 1) * P],
                                 hi[:, one(c), w:w + HID], lo[:, one(c), w:w + HID],
                                 first and t % 2 == 0, final, group=False)
            last.then_inc(down_done, 1)

        def pe_transposes(pe, blk, t, slot, routes):
            n = TPB * blk + t
            pe.wait_ge(xn_done, n + 1)
            if not (isinstance(n, int) and n == 0):
                pe.wait_ge(xT_lo_done, n)
            if not (isinstance(routes, int) and routes == 0):
                pe.wait_ge(wT_done, routes)
            for hc in range(HC):
                last = pe.transpose(misc[:, hc * P:(hc + 1) * P], xn[:, slot, hc * P:(hc + 1) * P],
                                    ident[:, :])
            last.then_inc(xT_ps, 1)

        def pe_logits(pe, f, b):
            r, e, o = f.r0 + b, NEXP[f.kind], RT0[f.kind]
            pe.wait_ge(xT_lo_done, TPB * (4 * f.phase + b + 1))
            if not (isinstance(r, int) and r == 0):
                pe.wait_ge(wT_done, r)
            for t in range(TPB):
                for hc in range(HC):
                    last = pe_split3(pe, misc[:, t * e:(t + 1) * e],
                                     xT_hi[:, hc, one(at(b)), t * P:(t + 1) * P],
                                     xT_lo[:, hc, one(at(b)), t * P:(t + 1) * P],
                                     rt_hi[:, o + hc * e:o + (hc + 1) * e],
                                     rt_lo[:, o + hc * e:o + (hc + 1) * e], hc == 0, hc == HC - 1)
            last.then_inc(logits_ps, 1)

        def pe_turn_weights(pe, f, b):
            pe.wait_ge(ws_done, f.r0 + b + 1)
            for t in range(TPB):
                last = pe.transpose(misc16[:, t * P:(t + 1) * P], ws[f.kind][:, t, :], ident16[:, :])
            last.then_inc(wT_ps, 1)

        def pe_ffn(pe, f):
            ti, tp, ri = SHAPE[f.kind]
            last_c = f.chunks - 1
            pe_logits(pe, f, 0)
            pe_gate_up(pe, f, 0, 0, 0)
            pe_turn_weights(pe, f, 0)
            pe.wait_ge(wT_done, f.r0 + 1)
            pe_spread(pe, f, 0, 0)
            with pe.Fori(0, NBLK) as b:
                nb = 4 * f.phase + b + 1
                pe_gate_up(pe, f, b, 1, 1)
                pe_spread(pe, f, b, 1)
                pe_down(pe, f, b, 0, 0, first=True)
                with pe.Fori(0, ti) as i:
                    for j in range(TCH):
                        c = i * TCH + (1 + j)
                        if 1 <= j <= tp:
                            pe_transposes(pe, nb, i * tp + (j - 1), j - 1, f.r0 + b + 1)
                        pe_gate_up(pe, f, b, c + 1, j % 2)
                        pe_spread(pe, f, b, c + 1)
                        pe_down(pe, f, b, c, (1 + j) % 2)
                with pe.If(b < NBLK - 1):
                    pe_logits(pe, f, b + 1)
                with pe.Fori(0, ri) as i:
                    for j in range(RCH):
                        c = i * RCH + (1 + ti * TCH + j)
                        pe_gate_up(pe, f, b, c + 1, j % 2)
                        pe_spread(pe, f, b, c + 1)
                        pe_down(pe, f, b, c, (1 + j) % 2)
                with pe.If(b < NBLK - 1):
                    pe_gate_up(pe, f, b + 1, 0, 0)
                    pe_turn_weights(pe, f, b + 1)
                pe_down(pe, f, b, last_c, 1, final=True)
                with pe.If(b < NBLK - 1):
                    pe.wait_ge(wT_done, f.r0 + b + 2)
                    pe_spread(pe, f, b + 1, 0)

        def pe_attention(pe):
            base = 4 * ATT_PHASE
            with pe.Fori(0, NBLK) as b:
                pe.wait_ge(xT_lo_done, TPB * (b + base + 1))
                banks = [gate_ps[0], gate_ps[1], up_ps[0], up_ps[1]]
                pe.wait_ge(attn_done, 2 * b + 2)
                for t in range(TPB):
                    for hc in range(HC):
                        last = pe_split3(pe, banks[t][:, :], xT_hi[:, hc, one(at(b)), t * P:(t + 1) * P],
                                         xT_lo[:, hc, one(at(b)), t * P:(t + 1) * P],
                                         w1_hi[:, C1 + hc, HID:3 * HID],
                                         w1_lo[:, C1 + hc, HID:3 * HID], hc == 0, hc == HC - 1)
                    last.then_inc(kv_ps_done, 1)
                pe.wait_ge(x_done, b + base + 4)
                for m in range(HC):
                    for hc in range(HC):
                        last = pe_split3(pe, y_ps[m][:, :], w1_hi[:, C1 + hc, m * P:(m + 1) * P],
                                         w1_lo[:, C1 + hc, m * P:(m + 1) * P],
                                         xT_hi[:, hc, one(at(b)), :], xT_lo[:, hc, one(at(b)), :],
                                         hc == 0, hc == HC - 1)
                    last.then_inc(q_ps_done, 1)
                pe.wait_ge(elu_done, 2 * b + 1)
                kv_bank = [wb_ps, gate_ps[0]]
                for t in range(TPB):
                    for g in range(2):
                        last = pe.matmul(kv_bank[g][:, 0:P + 1], k_pos[:, t, g * P:(g + 1) * P],
                                         v_sb[:, t, g * P:g * P + P + 1], start=t == 0, stop=t == TPB - 1)
                last.then_inc(sums_ps, 1)
                pe.wait_ge(elu_done, 2 * b + 2)
                pe.wait_ge(sums_done, b + 1)
                for g, (nb_, db_) in enumerate(((gate_ps[1], up_ps[0]), (up_ps[1], wb_ps))):
                    pe.matmul(db_[:, :], ks_m[:, g, :], q_pos[:, g, :], start=True, stop=True)
                    pe.matmul(nb_[:, :], kv_m[:, g, :], q_pos[:, g, :], start=True,
                              stop=True).then_inc(ratio_ps, 1)
                pe.wait_ge(attn_done, 2 * b + 4)
                for t in range(TPB):
                    for g in range(2):
                        last = pe.matmul(y_tile(t), attn[:, g, t * P:(t + 1) * P], o_w[:, g, :],
                                         start=g == 0, stop=g == 1)
                last.then_inc(o_ps_done, 1)
                for t in range(TPB):
                    pe_transposes(pe, b + base + 1, t, t % 2, 4)

        def pe_s4(pe):
            base = 4 * S4_PHASE
            for b in range(NBLK):
                pe.wait_ge(xT_lo_done, TPB * (b + base + 1))
                pe.wait_ge(x_done, b + base + 4)
                for t in range(TPB):
                    for hc in range(HC):
                        o = (t % 2) * HID + hc * P
                        for lag in range(b + 1):
                            last = pe_split3(pe, y_ps[t // 2][:, o:o + P],
                                             xT_hi[:, hc, b - lag, t * P:(t + 1) * P],
                                             xT_lo[:, hc, b - lag, t * P:(t + 1) * P],
                                             diag_hi[:, lag, hc, :], diag_lo[:, lag, hc, :],
                                             lag == 0, lag == b)
                last.then_inc(s4_ps_done, 1)
                for t in range(TPB):
                    pe_transposes(pe, base + b + 1, t, t % 2, 12)

        @block.tensor
        def _(pe):
            pe.wait_ge(ld_const, CONSTS)
            pe.wait_ge(ready, 1)
            for t in range(TPB):
                pe_transposes(pe, 0, t, t % 2, 0)
            pe.wait_ge(w_lo_done, C0)
            pe_ffn(pe, FFNS[0])
            pe.wait_ge(w_lo_done, C0 + LATE)
            pe_attention(pe)
            pe_ffn(pe, FFNS[1])
            pe_ffn(pe, FFNS[2])
            pe_s4(pe)
            pe_ffn(pe, FFNS[3])

        def act_silu(a, f, b, c, par):
            k = f.k0 + b * f.chunks + c
            a.wait_ge(gate_done, k + 1)
            a.wait_ge(p_done, k + 1)
            a.activation(silu[:, par, :], gate_ps[par][:, :], ACT.Silu, scale=XW).then_inc(silu_done, 1)

        def act_h_hi(a, f, b, c, par):
            k = f.k0 + b * f.chunks + c
            a.wait_ge(q_done, k + 3)
            a.wait_ge(down_done, k + 1)
            a.activation(h_hi[:, par, :], qbuf[:, par, :], ACT.Copy).then_inc(h_hi_done, 1)

        def act_chunk(a, f, b, c, par):
            act_silu(a, f, b, c, par)
            act_h_hi(a, f, b, c, par)

        def act_xT_hi(a, blk, dst, t):
            n = TPB * blk + t
            a.wait_ge(xT_ps, n + 1)
            a.activation(xT_hi[:, :, one(dst), bass.ds(t * P, P)].rearrange("p h o n -> p h (o n)"),
                         misc[:, 0:HID].rearrange("p (h n) -> p h n", h=HC), ACT.Copy).then_inc(xT_hi_done, 1)

        def act_route_exp(a, f, b):
            a.wait_ge(shifted, f.r0 + b + 1)
            if f.kind == 0:
                a.activation(ex[:, :, :], wf[:, :, :], ACT.Exp).then_inc(expd, 1)
            else:
                a.activation(ex[:, :, 0:E1], lb[1][:, :, 0:E1], ACT.Exp, scale=-1.0).then_inc(expd, 1)

        def act_weights_T(a, f, b):
            a.wait_ge(wT_ps, f.r0 + b + 1)
            a.activation(wT[:, one(odd(b)), :], misc16[:, 0:BLK], ACT.Copy).then_inc(wT_done, 1)

        def act_weights_hi(a, dst, n, s, count):
            a.wait_ge(ld_w[s], 16 * count)
            a.activation(dst[:, one(n), :], stage[:, s, :], ACT.Copy, scale=WS).then_inc(w_hi_done, 1)

        def act_ffn(a, f):
            ti, tp, ri = SHAPE[f.kind]
            last_c = f.chunks - 1
            act_route_exp(a, f, 0)
            act_silu(a, f, 0, 0, 0)
            act_weights_T(a, f, 0)
            act_h_hi(a, f, 0, 0, 0)
            with a.Fori(0, NBLK) as b:
                nb = 4 * f.phase + b + 1
                act_chunk(a, f, b, 1, 1)
                with a.Fori(0, ti) as i:
                    for j in range(TCH):
                        c = i * TCH + (1 + j)
                        if 2 <= j <= tp + 1:
                            act_xT_hi(a, nb, nxt(b), i * tp + (j - 2))
                        act_chunk(a, f, b, c + 1, j % 2)
                    if f.late:
                        act_late(a, b, i)
                with a.If(b < NBLK - 1):
                    act_route_exp(a, f, b + 1)
                with a.Fori(0, ri) as i:
                    for j in range(RCH):
                        act_chunk(a, f, b, i * RCH + (2 + ti * TCH + j), j % 2)
                with a.If(b < NBLK - 1):
                    act_silu(a, f, b + 1, 0, 0)
                    act_weights_T(a, f, b + 1)
                    act_h_hi(a, f, b + 1, 0, 0)

        def act_late(a, b, i):
            n = b * TPB + i
            a.wait_ge(ld_w[0], n * 16 + 16 * (C0 // NSTAGE + 1))
            a.activation(w1_hi[:, one(n), :], stage[:, 0, :], ACT.Copy, scale=WS).then_inc(w_hi_done, 1)

        def act_attention(a):
            base = 4 * ATT_PHASE
            with a.Fori(0, NBLK) as b:
                a.wait_ge(elu_min, 2 * b + 1)
                a.activation(k_pos[:, :, :], k_pos[:, :, :], ACT.Exp).then_inc(elu_exp, 1)
                for m in range(HC):
                    a.wait_ge(q_ps_done, 2 * b + m + 1)
                    a.activation(q_raw[:, m, :], y_ps[m][:, :], ACT.Identity, scale=XW,
                                 bias=small[:, PQB + m:PQB + m + 1]).then_inc(q_raw_done, 1)
                a.wait_ge(elu_min, 2 * b + 2)
                a.activation(q_pos[:, :, :], q_pos[:, :, :], ACT.Exp).then_inc(elu_exp, 1)
                for t in range(TPB):
                    act_xT_hi(a, b + base + 1, nxt(b), t)

        def act_s4(a):
            base = 4 * S4_PHASE
            with a.Fori(0, NBLK) as b:
                for t in range(TPB):
                    act_xT_hi(a, b + base + 1, nxt(b), t)

        @block.scalar
        def _(a):
            for s in (silu_done, h_hi_done):
                a.sem_inc(s, 2)
            a.wait_ge(ld_const, CONSTS)
            a.activation(S["dt"], small[:, PDT:PDT + HC], ACT.Exp).then_inc(par_act, 1)
            a.activation(S["are"], small[:, PAR:PAR + 16], ACT.Exp).then_inc(par_act, 1)
            a.wait_ge(par_dve, PAR_A)
            a.activation(S["th"], S["a"], ACT.Tanh, scale=0.5).then_inc(par_act, 1)
            a.wait_ge(par_dve, PAR_T)
            a.activation(S["sin"], S["ang"], ACT.Sin).then_inc(par_act, 1)
            a.activation(S["sh"], S["ang"], ACT.Sin, scale=0.5).then_inc(par_act, 1)
            for t in range(TPB):
                act_xT_hi(a, 0, 0, t)
            with a.Fori(0, C0 // NSTAGE) as i:
                for s in range(NSTAGE):
                    act_weights_hi(a, w0_hi, i * NSTAGE + s, s, i + 1)
            act_ffn(a, FFNS[0])
            act_attention(a)
            act_ffn(a, FFNS[1])
            act_ffn(a, FFNS[2])
            act_s4(a)
            act_ffn(a, FFNS[3])

        class Chain:

            def __init__(self, eng, s, base):
                self.eng, self.s, self.n = eng, s, base

            def step(self, ins):
                ins.then_inc(self.s, 1)
                self.n = self.n + 1

            def then(self, ins):
                self.step(ins)
                self.eng.wait_ge(self.s, self.n)

            def then_alone(self, ins):
                self.then(ins)
                self.eng.sem_inc(waited, 1)

        def dve_s4_parameters(v):
            ch = Chain(v, par_dve, 0)
            tt = v.tensor_tensor
            v.wait_ge(par_act, 2)

            def per_state(ap):
                return ap.rearrange("p (h n) -> p h n", h=HC)

            dtb = S["dt"].unsqueeze(2).to_broadcast([P, HC, NS4])
            ch.then(v.tensor_scalar(S["aren"], S["are"], -1.0, None, ALU.mult))
            ch.then(tt(per_state(S["a"]), per_state(S["aren"]), dtb, ALU.mult))
            assert ch.n == PAR_A
            ai = small[:, PAI:PAI + 16]
            ch.then(tt(per_state(S["ang0"]), per_state(ai), dtb, ALU.mult))
            magic = 12582912.0
            ch.then(v.tensor_scalar(S["turn"], S["ang0"], 1.0 / (2 * np.pi), magic, ALU.mult, ALU.add))
            ch.then(v.tensor_scalar(S["turn"], S["turn"], magic, None, ALU.subtract))
            c1 = 6.28125
            c2 = 2 * np.pi - c1
            ch.then(v.scalar_tensor_tensor(S["ang0"], S["turn"], -c1, S["ang0"], ALU.mult, ALU.add))
            ch.then(v.scalar_tensor_tensor(S["ang0"], S["turn"], -c2, S["ang0"], ALU.mult, ALU.add))
            ch.then(v.tensor_scalar(S["ang"], S["ang0"], 3.1415925, -3.1415925, ALU.min, ALU.max))
            ch.then(v.tensor_copy(S["nre"], S["ang"]))
            assert ch.n == PAR_T
            v.wait_ge(par_act, 5)
            ch.then(v.tensor_scalar(S["omt"], S["th"], -1.0, 1.0, ALU.mult, ALU.add))
            ch.then(v.reciprocal(S["omt"], S["omt"]))
            ch.then(v.scalar_tensor_tensor(S["em1"], S["th"], 2.0, S["omt"], ALU.mult, ALU.mult))
            ch.then(v.tensor_scalar(S["ea"], S["em1"], 1.0, None, ALU.add))
            ch.then(v.scalar_tensor_tensor(S["cm1"], S["sh"], -2.0, S["sh"], ALU.mult, ALU.mult))
            ch.then(v.tensor_scalar(S["cos"], S["cm1"], 1.0, None, ALU.add))
            ch.then(tt(S["wre"], S["ea"], S["cos"], ALU.mult))
            ch.then(tt(S["wim"], S["ea"], S["sin"], ALU.mult))
            ch.then(tt(S["t1"], S["em1"], S["cos"], ALU.mult))
            ch.then(tt(S["ere"], S["t1"], S["cm1"], ALU.add))

            def product(re, im, are, aim, bre, bim):
                ch.then(tt(S["t1"], aim, bim, ALU.mult))
                ch.then(tt(S["t2"], are, bre, ALU.mult))
                ch.then(tt(re, S["t2"], S["t1"], ALU.subtract))
                ch.then(tt(S["t1"], are, bim, ALU.mult))
                ch.then(tt(S["t2"], aim, bre, ALU.mult))
                ch.then(tt(im, S["t2"], S["t1"], ALU.add))

            ch.then(tt(S["t1"], S["aren"], S["aren"], ALU.mult))
            ch.then(tt(S["t2"], ai, ai, ALU.mult))
            ch.then(tt(S["inv"], S["t1"], S["t2"], ALU.add))
            ch.then(v.reciprocal(S["inv"], S["inv"]))
            ch.then(v.tensor_scalar(S["nim"], ai, -1.0, None, ALU.mult))
            product(S["fre"], S["fim"], S["ere"], S["wim"], S["aren"], S["nim"])
            ch.then(tt(S["fre"], S["fre"], S["inv"], ALU.mult))
            ch.then(tt(S["fim"], S["fim"], S["inv"], ALU.mult))
            product(S["cre"], S["cim"], small[:, PCR:PCR + 16], small[:, PCI:PCI + 16], S["fre"], S["fim"])
            for lag in range(NBLK):
                kc = S[f"kc{lag}"]
                ch.then(v.tensor_reduce(kc, per_state(S["cre"]), AXX, ALU.add))
                ch.then(v.tensor_scalar(kc, kc, 2.0 * WS, None, ALU.mult))
                if lag == 0:
                    ch.then(v.scalar_tensor_tensor(kc, small[:, PD:PD + HC], WS, kc, ALU.mult, ALU.add))
                for hc in range(HC):
                    ch.then(v.tensor_scalar(diag_hi[:, lag, hc, :], ident[:, :], kc[:, hc:hc + 1], None,
                                            ALU.mult))
                    ch.then(v.scalar_tensor_tensor(diag_lo[:, lag, hc, :], ident[:, :], kc[:, hc:hc + 1],
                                                   diag_hi[:, lag, hc, :], ALU.mult, ALU.subtract))
                if lag < NBLK - 1:
                    product(S["nre"], S["nim"], S["cre"], S["cim"], S["wre"], S["wim"])
                    ch.then(v.tensor_copy(S["cre"], S["nre"]))
                    ch.then(v.tensor_copy(S["cim"], S["nim"]))

        def dve_stats(v, blk, src):
            ch = Chain(v, stats, blk * 3)
            if not (isinstance(blk, int) and blk == 0):
                v.wait_ge(x_done, blk + 1)
            for t in range(TPB):
                ins = v.bn_stats(bn[:, t, :], x[:, one(src * TPB + t), :])
            ch.then_alone(ins)
            for t in range(TPB):
                ins = v.bn_aggr(mv[:, t, :], bn[:, t, :])
            ch.then(ins)
            ch.step(v.tensor_scalar(ve[:, :], mv[:, :, 1], EPS, 1.0 / (XS * XS), ALU.add, ALU.mult))

        def dve_normalise(v, blk, src, t, slot, slots=2):
            n = TPB * blk + t
            v.wait_ge(rstd_done, blk + 1)
            if not (isinstance(n, int) and n < slots):
                v.wait_ge(xT_ps, n + (1 - slots))
            v.tensor_scalar(xn[:, slot, :], x[:, one(src * TPB + t), :], mv[:, one(t), 0:1],
                            rstd[:, one(t)], ALU.subtract, ALU.mult).then_inc(xn_done, 1)

        def dve_xT_lo(v, blk, dst, t):
            n = TPB * blk + t
            v.wait_ge(xT_hi_done, n + 1)
            sl = (slice(None), slice(None), one(dst), bass.ds(t * P, P))
            v.tensor_tensor(xT_lo[sl].rearrange("p h o n -> p h (o n)"),
                            misc[:, 0:HID].rearrange("p (h n) -> p h n", h=HC),
                            xT_hi[sl].rearrange("p h o n -> p h (o n)"),
                            ALU.subtract).then_inc(xT_lo_done, 1)

        def dve_tiles(v, blk, src):
            dve_normalise(v, blk, src, 0, 0)
            for t in range(TPB):
                if t + 1 < TPB:
                    dve_normalise(v, blk, src, t + 1, (t + 1) % 2)
                dve_xT_lo(v, blk, src, t)

        def route_steps(kind):
            return 7 if kind == 0 else 9

        def dve_route_choose(v, f, b):
            e, k, kind = NEXP[f.kind], NTOP[f.kind], f.kind
            rl = b + (4 if f.phase in (2, 5) else 0)
            ch = Chain(v, route_dve[kind], rl * route_steps(kind))
            v.wait_ge(logits_ps, f.r0 + b + 1)
            ch.then_alone(v.tensor_scalar(lb[kind][:, :, 0:e], misc[:, 0:TPB * e].rearrange("p (t e) -> p t e", t=TPB),
                                    XW, None, ALU.mult))
            for t in range(TPB):
                ins = v.max(m8[:, t, :], lb[kind][:, t, 0:e])
            ch.then(ins)
            if kind == 0:
                v.tensor_tensor(wf[:, :, :], lb[0][:, :, 0:e],
                                m8[:, :, 0:1].to_broadcast([P, TPB, e]), ALU.subtract).then_inc(shifted, 1)
            else:
                v.tensor_scalar(m8[:, :, 6:8], m8[:, :, 6:8], 1.0, None, ALU.mult).then_inc(shifted, 1)
            ch.then_alone(v.tensor_copy(top[kind][:, :, 0:k], m8[:, :, 0:k]))
            for t in range(TPB):
                ins = v.match_replace(rb[kind][:, t, :], top[kind][:, t, :], lb[kind][:, t, :], TAKEN)
            ch.step(ins)

        def dve_route_weigh(v, f, b):
            e, kind = NEXP[f.kind], f.kind
            rl = b + (4 if f.phase in (2, 5) else 0)
            ch = Chain(v, route_dve[kind], rl * route_steps(kind) + 4)
            v.wait_ge(route_dve[kind], ch.n)
            v.wait_ge(expd, f.r0 + b + 1)
            prob = ex[:, :, 0:e]
            if kind == 1:
                ch.then(v.tensor_scalar(prob, prob, 1.0, None, ALU.add))
                ch.then(v.reciprocal(prob, prob))
            w = wf[:, :, 0:e]
            ch.then(v.scalar_tensor_tensor(w, rb[kind][:, :, 0:e], TAKEN, prob, ALU.is_equal, ALU.mult))
            ch.then(v.tensor_reduce(rsum[:, :], w, AXX, ALU.add))
            if kind == 1:
                v.tensor_scalar(rsum[:, :], rsum[:, :], 1e-20, None, ALU.add).then_inc(y_tmp, 1)
                v.wait_ge(y_tmp, rl + 1)
            ch.then(v.reciprocal(rrec[:, :], rsum[:, :]))
            scale = RS * HALF * (1.0 if kind == 0 else ROUTE1_SCALE)
            if not (isinstance(b, int) and f.r0 + b == 0):
                v.wait_ge(wT_ps, f.r0 + b)
            v.tensor_tensor(w, w, rrec[:, :].unsqueeze(2).to_broadcast([P, TPB, e]), ALU.mult).then_inc(
                w_ready, 1)
            v.wait_ge(w_ready, 2 * (f.r0 + b) + 1)
            v.tensor_scalar(ws[kind][:, :, 0:e], w, scale, None, ALU.mult).then_inc(w_ready, 1)
            v.wait_ge(w_ready, 2 * (f.r0 + b) + 2)
            v.scalar_tensor_tensor(ws[kind][:, :, LO_ROW:LO_ROW + e], w, scale, ws[kind][:, :, 0:e],
                                   ALU.mult, ALU.subtract).then_inc(ws_done, 1)


        def dve_chunk(v, f, b, c, par):
            k = f.k0 + b * f.chunks + c
            v.wait_ge(silu_done, k + 3)
            v.wait_ge(up_done, k + 1)
            v.scalar_tensor_tensor(pbuf, up_ps[par][:, :], P_SCALE, silu[:, par, :], ALU.mult,
                                   ALU.mult).then_inc(p_done, 1)
            v.wait_ge(p_done, k + 3)
            v.wait_ge(wb_done, k + 1)
            v.wait_ge(h_hi_done, k + 1)
            v.tensor_tensor(qbuf[:, par, :], pbuf, wb_ps[:, :], ALU.mult).then_inc(q_done, 1)
            v.wait_ge(h_hi_done, k + 3)
            v.tensor_tensor(h_lo[:, par, :], qbuf[:, par, :], h_hi[:, par, :],
                            ALU.subtract).then_inc(h_lo_done, 1)

        def dve_add_y(v, phase, b, scale):
            for m in range(2):
                xs = x[:, bass.ds(b * TPB + 2 * m, 2), :].rearrange("p t n -> p (t n)")
                ins = v.scalar_tensor_tensor(xs, y_ps[m][:, :], scale, xs, ALU.mult, ALU.add)
            ins.then_inc(x_done, 1)

        def dve_weights_lo(v, dst_hi, dst_lo, n, s, count):
            v.wait_ge(w_hi_done, count)
            v.scalar_tensor_tensor(dst_lo[:, one(n), :], stage[:, s, :], WS, dst_hi[:, one(n), :],
                                   ALU.mult, ALU.subtract).then_inc(w_lo_done, 1)

        def dve_ffn(v, f):
            ti, tp, ri = SHAPE[f.kind]
            last_c = f.chunks - 1
            dve_route_choose(v, f, 0)
            dve_route_weigh(v, f, 0)
            dve_chunk(v, f, 0, 0, 0)
            with v.Fori(0, NBLK) as b:
                nb = 4 * f.phase + b + 1
                dve_stats(v, nb, nxt(b))
                dve_chunk(v, f, b, 1, 1)
                with v.Fori(0, ti) as i:
                    for j in range(TCH):
                        c = i * TCH + (1 + j)
                        if j < tp:
                            dve_normalise(v, nb, nxt(b), i * tp + j, j, tp)
                        if 2 <= j <= tp + 1:
                            dve_xT_lo(v, nb, nxt(b), i * tp + (j - 2))
                        dve_chunk(v, f, b, c + 1, j % 2)
                    if f.late:
                        n = b * TPB + i
                        dve_weights_lo(v, w1_hi, w1_lo, n, 0, n + (C0 + 1))
                with v.If(b < NBLK - 1):
                    dve_route_choose(v, f, b + 1)
                with v.Fori(0, ri) as i:
                    for j in range(RCH):
                        dve_chunk(v, f, b, i * RCH + (2 + ti * TCH + j), j % 2)
                with v.If(b < NBLK - 1):
                    dve_route_weigh(v, f, b + 1)
                    dve_chunk(v, f, b + 1, 0, 0)
                v.wait_ge(down_done, f.k0 + b * f.chunks + (f.chunks + 2))
                dve_add_y(v, f.phase, b, 1.0 / (HS * WS))

        def dve_attention(v):
            base = 4 * ATT_PHASE
            v.wait_ge(ld_att, 32)
            for t in range(TPB):
                ins = v.memset(v_sb[:, t, P:P + 1], 1.0)
            ins.then_inc(ready, 1)
            with v.Fori(0, NBLK) as b:
                for t in range(TPB):
                    bank = (gate_ps[0], gate_ps[1], up_ps[0], up_ps[1])[t]
                    v.wait_ge(kv_ps_done, TPB * b + t + 1)
                    v.scalar_tensor_tensor(k_raw[:, t, :], bank[:, 0:HID], XW, kv_b[:, 0:HID],
                                           ALU.mult, ALU.add)
                    v.scalar_tensor_tensor(
                        v_sb[:, t, :].rearrange("p (g n) -> p g n", g=2)[:, :, 0:P] if False else v_sb[:, t, 0:P],
                        bank[:, HID:HID + P], XW, kv_b[:, HID:HID + P], ALU.mult, ALU.add)
                    v.scalar_tensor_tensor(v_sb[:, t, P + 1:2 * P + 1], bank[:, HID + P:2 * HID], XW,
                                           kv_b[:, HID + P:2 * HID], ALU.mult, ALU.add).then_inc(k_raw_done, 1)
                v.wait_ge(k_raw_done, TPB * b + TPB)
                v.tensor_scalar(k_pos[:, :, :], k_raw[:, :, :], 0.0, None, ALU.min).then_inc(elu_min, 1)
                dve_stats(v, b + base + 1, nxt(b))
                for m in range(HC):
                    v.wait_ge(q_raw_done, HC * b + m + 1)
                    ins = v.tensor_scalar(q_pos[:, m, :], q_raw[:, m, :], 0.0, None, ALU.min)
                ins.then_inc(elu_min, 1)
                v.wait_ge(elu_exp, 2 * b + 1)
                v.scalar_tensor_tensor(k_pos[:, :, :], k_raw[:, :, :], 0.0, k_pos[:, :, :], ALU.max,
                                       ALU.add).then_inc(elu_done, 1)
                v.wait_ge(elu_exp, 2 * b + 2)
                v.scalar_tensor_tensor(q_pos[:, :, :], q_raw[:, :, :], 0.0, q_pos[:, :, :], ALU.max,
                                       ALU.add).then_inc(elu_done, 1)
                v.wait_ge(sums_ps, b + 1)
                v.tensor_tensor(kv_m[:, 0, :], wb_ps[:, 0:P], mask[:, :], ALU.mult)
                v.tensor_scalar(ks_m[:, 0, :], mask[:, :], wb_ps[:, P:P + 1], None, ALU.mult)
                v.tensor_tensor(kv_m[:, 1, :], gate_ps[0][:, 1:P + 1], mask[:, :], ALU.mult)
                v.tensor_scalar(ks_m[:, 1, :], mask[:, :], gate_ps[0][:, 0:1], None,
                                ALU.mult).then_inc(sums_done, 1)
                for g, (num, dn) in enumerate(((gate_ps[1], up_ps[0]), (up_ps[1], wb_ps))):
                    ch = Chain(v, ratio_dve, 4 * b + 2 * g)
                    v.wait_ge(ratio_ps, 2 * b + g + 1)
                    if g:
                        v.wait_ge(attn_done, 2 * b + 3)
                    ch.then(v.tensor_scalar(den, dn[:, :], ATT_EPS, None, ALU.add))
                    ch.then(v.reciprocal(den, den))
                    v.tensor_tensor(attn[:, g, :], num[:, :], den, ALU.mult).then_inc(attn_done, 1)
                v.wait_ge(o_ps_done, b + 1)
                obb = o_b.unsqueeze(1).to_broadcast([P, TPB, HID])
                xb = x[:, bass.ds(b * TPB, TPB), :]
                v.tensor_tensor(xb, xb, obb, ALU.add).then_inc(y_add, 1)
                v.wait_ge(y_add, b + 1)
                dve_add_y(v, ATT_PHASE, b, 1.0)
                dve_tiles(v, b + base + 1, nxt(b))


        def dve_s4(v):
            base = 4 * S4_PHASE
            with v.Fori(0, NBLK) as b:
                dve_stats_after = b + base + 1
                v.wait_ge(s4_ps_done, b + 1)
                dve_add_y(v, S4_PHASE, b, XW)
                dve_stats(v, dve_stats_after, nxt(b))
                dve_tiles(v, dve_stats_after, nxt(b))

        @block.vector
        def _(v):
            for s in (p_done, q_done, h_lo_done):
                v.sem_inc(s, 2)
            v.sem_inc(down_done, 2)
            v.sem_inc(attn_done, 2)
            ch = Chain(v, dve_init, 0)
            for s in range(2):
                ch.step(v.memset(ws[s][:, :, :].bitcast(F32), 0.0))
            ch.step(v.memset(sel[64:P, :].bitcast(F32), 0.0))
            ch.step(v.memset(mhalf[:, :], -0.5))
            for s, (e, k) in enumerate(((E0, TOP0), (E1, TOP1))):
                ch.step(v.memset(lb[s][:, :, e:e + 8 - k], NEVER))
                ch.step(v.memset(top[s][:, :, k:8], NEVER))
            v.wait_ge(dve_init, ch.n)
            ch.step(v.memset(ws[1][:, :, E1:R1], RS * HALF))
            v.wait_ge(ld_const, CONSTS)
            ch.step(v.tensor_copy(ident16[:, :], ident[:, :]))
            ch.then(v.tensor_scalar(rt_hi[:, :], small[:, PR0:PCOLS], WS, None, ALU.mult))
            ch.then(v.scalar_tensor_tensor(rt_lo[:, :], small[:, PR0:PCOLS], WS, rt_hi[:, :], ALU.mult,
                                           ALU.subtract))
            v.sem_inc(ready, 1)
            dve_s4_parameters(v)
            v.wait_ge(ld_x0, 16)
            dve_stats(v, 0, 0)
            dve_tiles(v, 0, 0)
            v.wait_ge(ld_x, 16)
            v.sem_inc(x_done, NBLK)
            with v.Fori(0, C0 // NSTAGE) as i:
                for s in range(NSTAGE):
                    n = i * NSTAGE + s
                    dve_weights_lo(v, w0_hi, w0_lo, n, s, n + 1)
            dve_ffn(v, FFNS[0])
            dve_attention(v)
            dve_ffn(v, FFNS[1])
            dve_ffn(v, FFNS[2])
            dve_s4(v)
            dve_ffn(v, FFNS[3])


        @block.gpsimd
        def _(pool):
            def rsqrt(blk):
                pool.wait_ge(stats, 3 * blk + 3)
                pool.tensor_tensor(rstd[:, :], ve[:, :], mhalf[:, :], ALU.pow).then_inc(rstd_done, 1)

            pool.wait_ge(dve_init, 8)
            rsqrt(0)
            with pool.Fori(1, NBLK * 6 + 1) as i:
                rsqrt(i)

        CONSTS_N = 4
        @block.sync
        def _(sp):
            sp.dma_start(small[:, :], small_in).then_inc(ld_const, 16)
            sp.dma_start(x[:, 0:TPB, :], x_in[:, 0:TPB, :]).then_inc(ld_x0, 16)
            sp.dma_start(ident[:, :], ident_in).then_inc(ld_const, 16)
            sp.dma_start(mask[:, :], mask_in).then_inc(ld_const, 16)
            sp.dma_start(sel[0:64, :], sel_in).then_inc(ld_const, 16)
            sp.dma_start(x[:, TPB:, :], x_in[:, TPB:, :]).then_inc(ld_x, 16)
            for s in range(NSTAGE):
                sp.dma_start(stage[:, s, :], w0_in[s]).then_inc(ld_w[s], 16)
            with sp.Fori(1, C0 // NSTAGE) as i:
                for s in range(NSTAGE):
                    n = i * NSTAGE + s
                    sp.wait_ge(w_lo_done, n + (1 - NSTAGE))
                    sp.dma_start(stage[:, s, :], w0_in[one(n)].rearrange("o p n -> (o p) n")).then_inc(
                        ld_w[s], 16)
            with sp.Fori(0, LATE) as n:
                sp.wait_ge(w_lo_done, n + C0)
                sp.dma_start(stage[:, 0, :], late_in[one(n)].rearrange("o p n -> (o p) n")).then_inc(
                    ld_w[0], 16)
            sp.dma_start(o_w[:, :, :], ow_in).then_inc(ld_att, 16)
            sp.wait_ge(w_lo_done, C0 + LATE)
            sp.dma_start(work[:, KVB:KVB + 768], kvb_in.to_broadcast([P, 768])).then_inc(ld_att, 16)
            base = 4 * 5 + 4
            with sp.Fori(0, NBLK) as b:
                sp.wait_ge(x_done, b + base + 1)
                sp.dma_start(out[:, bass.ds(b * TPB, TPB), :], x[:, bass.ds(b * TPB, TPB), :]).then_inc(
                    stored, 16)
            sp.wait_ge(stored, 16 * NBLK)


CONSTS = 64


def kernel(**inputs):
    import numpy as _np
    import concourse.bacc as _bacc
    from concourse import mybir as _mybir
    from concourse.bass_utils import run_bass_kernel_spmd as _run

    f32 = _np.float32
    a = {k: _np.asarray(v) for k, v in inputs.items()}

    def chunks_of_rows(w, n):
        pad = _np.zeros((n * P - w.shape[0], w.shape[1]), w.dtype)
        w = _np.concatenate([w, pad], 0).reshape(n, P, HC, P)
        return w.transpose(0, 3, 2, 1).reshape(n, P, HC * P)

    def chunks_of_down(w, n):
        pad = _np.zeros((n * P - w.shape[0], w.shape[1]), w.dtype)
        return _np.concatenate([w, pad], 0).reshape(n, P, HID)

    def rows(w):
        return w.reshape(-1, w.shape[-1])

    w0 = _np.concatenate([
        chunks_of_rows(rows(a["L0_ffn_gate_w"]), C0), chunks_of_rows(rows(a["L0_ffn_up_w"]), C0),
        chunks_of_down(rows(a["L0_ffn_down_w"].transpose(0, 2, 1)), C0)], 2)
    gate1 = _np.concatenate([rows(a["L1_ffn_exp_wg"]), a["L1_ffn_shared_wg"]], 0)
    up1 = _np.concatenate([rows(a["L1_ffn_exp_wu"]), a["L1_ffn_shared_wu"]], 0)
    down1 = _np.concatenate([rows(a["L1_ffn_exp_wd"].transpose(0, 2, 1)), a["L1_ffn_shared_wd"].T], 0)
    w1 = _np.concatenate([chunks_of_rows(gate1, C1), chunks_of_rows(up1, C1), chunks_of_down(down1, C1)], 2)
    qkv = _np.concatenate([a["L0_attn_q_w"].T, a["L0_attn_k_w"].T, a["L0_attn_v_w"].T], 1).reshape(HC, P, 3 * HID)
    late = _np.concatenate([w1, qkv], 0)

    def halves(v):
        v = v.reshape(HC, P, -1)
        return v.transpose(1, 0, 2).reshape(P, -1)

    small = _np.concatenate([
        halves(a["L0_attn_q_b"]), halves(a["L1_attn_log_dt"]), halves(a["L1_attn_D_param"]),
        halves(a["L1_attn_A_real_log"]), halves(a["L1_attn_A_imag"]), halves(a["L1_attn_C_re"]),
        halves(a["L1_attn_C_im"]), halves(a["L0_ffn_router_w"].T), halves(a["L1_ffn_gate_w"].T)], 1)
    kvb = _np.concatenate([a["L0_attn_k_b"], a["L0_attn_v_b"], a["L0_attn_o_b"]]).reshape(1, 3 * HID)
    ow = a["L0_attn_o_w"].T.reshape(HC, P, HID).transpose(1, 0, 2)
    ident = _np.eye(P, dtype=f32)
    mask = _np.kron(_np.eye(P // HD), _np.ones((HD, HD))).astype(f32)
    sel = _np.zeros((64, (C0 + C1) * P), _np.float16)
    for e in range(E0):
        sel[e, e * I0:(e + 1) * I0] = sel[LO_ROW + e, e * I0:(e + 1) * I0] = 1
    for e in range(R1):
        o = C0 * P + e * I1
        sel[e, o:o + I1] = sel[LO_ROW + e, o:o + I1] = 1
    xin = a["L0_attn_hidden_states"].reshape(NBLK * TPB, P, HID).transpose(1, 0, 2)

    given = dict(x=xin, w0=w0, late=late, small=small, kvb=kvb, ow=ow, sel=sel, ident=ident, mask=mask)
    nc = _bacc.Bacc("TRN2", target_bir_lowering=False, num_devices=1)
    arrays = {f"{n}_dram": _np.ascontiguousarray(v) for n, v in given.items()}
    d = {n: nc.dram_tensor(f"{n}_dram", arrays[f"{n}_dram"].shape,
                           _mybir.dt.from_np(arrays[f"{n}_dram"].dtype), kind="ExternalInput").ap()
         for n in given}
    out = nc.dram_tensor("out_0_dram", (P, NBLK * TPB, HID), F32, kind="ExternalOutput").ap()
    build(nc, d["x"], d["w0"], d["late"], d["small"], d["kvb"], None, d["ow"], d["sel"], d["ident"],
          d["mask"], out)
    r = _run(nc, [arrays], core_ids=[0])
    return r.results[0]["out_0_dram"].transpose(1, 0, 2).reshape(NBLK, BLK, HID)
```

```python
from contextlib import ExitStack, nullcontext
from collections import namedtuple

import numpy as np
import concourse.bass as bass
from concourse import mybir

F32 = mybir.dt.float32
F16 = mybir.dt.float16
ALU = mybir.AluOpType
ACT = mybir.ActivationFunctionType
AXX = mybir.AxisListType.X

P = 128
HID = 256
HC = HID // P
NBLK = 4
BLK = 512
TPB = BLK // P
E0, I0, TOP0 = 32, 96, 4
E1, I1, TOP1, SHARED1 = 8, 176, 2, 352
C0 = E0 * I0 // P
C1 = -(-(E1 * I1 + SHARED1) // P)
R1 = E1 + SHARED1 // I1
WCOLS = HC * P + HC * P + HID
QCHUNKS = 2
LATE = C1 + QCHUNKS
UNIT = 1024
UNITS = LATE * WCOLS // UNIT
HEADS, HD = 16, 16
NS4 = 8
EPS = 1e-5
ATT_EPS = 1e-6

XS = 16.0
WS = 64.0
RS = 256.0
HS = 4.0
XW = 1.0 / (XS * WS)
P_SCALE = HS / (XS * WS * RS)
HALF = 0.5
ROUTE1_SCALE = 2.5
NEVER = -1e30
TAKEN = -3e38
SENT0, SENT1 = 8 - TOP0, 8 - TOP1
LO_ROW = 32

PQB, PDT, PD = 0, 2, 4
PAR, PAI, PCR, PCI = 6, 22, 38, 54
PR0 = 70
PR1 = PR0 + HC * E0
PCOLS = PR1 + HC * E1

Ffn = namedtuple("Ffn", "phase chunks k0 r0 kind late")


def build(nc, x_in, w0_in, late_in, small_in, bias_in, ow_in, sel_in, ident_in, mask_in, out):
    ctx = ExitStack()
    with ctx:
        def sb(name, shape, dt):
            return ctx.enter_context(nc.sbuf_tensor(name, shape, dt))

        def pb(name, shape, dt):
            return ctx.enter_context(nc.psum_tensor(name, shape, dt))

        def sem(name):
            return ctx.enter_context(nc.semaphore(name))

        x = sb("x", [P, NBLK * TPB, HID], F32)
        w0_hi = sb("w0_hi", [P, C0, WCOLS], F16)
        w0_lo = sb("w0_lo", [P, C0, WCOLS], F16)
        w1_hi = sb("w1_hi", [P, LATE, WCOLS], F16)
        w1_lo = sb("w1_lo", [P, LATE, WCOLS], F16)
        sel = sb("sel", [P, (C0 + C1 + 2) * P], F16)
        xT_hi = sb("xT_hi", [P, HC, NBLK, BLK], F16)
        xT_lo = sb("xT_lo", [P, HC, NBLK, BLK], F16)
        xn = sb("xn", [P, 2, HID], F32)
        wT = sb("wT", [P, 2, BLK], F16)
        ws = [sb("ws0", [P, TPB, P], F16), sb("ws1", [P, TPB, P], F16)]
        diag_hi = sb("diag_hi", [P, NBLK, HC, P], F16)
        diag_lo = sb("diag_lo", [P, NBLK, HC, P], F16)
        o_w = sb("o_w", [P, HC, HID], F32)
        ident = sb("ident", [P, P], F32)
        ident16 = sb("ident16", [P, P], F16)
        mask = sb("mask", [P, P], F32)
        kv_m = sb("kv_m", [P, 2, P], F32)
        ks_m = sb("ks_m", [P, 2, P], F32)
        small = sb("small", [P, PCOLS], F32)
        rt_hi = sb("rt_hi", [P, PCOLS - PR0], F16)
        rt_lo = sb("rt_lo", [P, PCOLS - PR0], F16)
        bn = sb("bn", [P, TPB, 6], F32)
        mv = sb("mv", [P, TPB, 2], F32)
        ve = sb("ve", [P, TPB], F32)
        mhalf = sb("mhalf", [P, TPB], F32)
        minus1 = sb("minus1", [P, 16], F32)
        eps_t = sb("eps_t", [P, 1], F32)
        rstd = sb("rstd", [P, TPB], F32)
        lb = [sb("lb0", [P, TPB, E0 + SENT0], F32), sb("lb1", [P, TPB, E1 + SENT1], F32)]
        rb = [sb("rb0", [P, TPB, E0 + SENT0], F32), sb("rb1", [P, TPB, E1 + SENT1], F32)]
        m8 = sb("m8", [P, TPB, 8], F32)
        top = [sb("top0", [P, TPB, 8], F32), sb("top1", [P, TPB, 8], F32)]
        ex = sb("ex", [P, TPB, E0], F32)
        wf = sb("wf", [P, TPB, E0], F32)
        rsum = sb("rsum", [P, TPB], F32)
        rrec = sb("rrec", [P, TPB], F32)

        WORK = 5896
        work = sb("work", [P, WORK], F32)
        silu = work[:, 0:1024].rearrange("p (a n) -> p a n", a=2)
        pbuf = work[:, 1024:1536]
        qbuf = work[:, 1536:2560].rearrange("p (a n) -> p a n", a=2)
        h_hi = work[:, 2560:3072].bitcast(F16).rearrange("p (a n) -> p a n", a=2)
        h_lo = work[:, 3072:3584].bitcast(F16).rearrange("p (a n) -> p a n", a=2)
        NSTAGE = 2
        STAGE = 3584
        stage = work[:, STAGE:STAGE + NSTAGE * WCOLS].rearrange("p (a n) -> p a n", a=NSTAGE)
        stage_late = work[:, STAGE:STAGE + UNIT]
        S4_AT = STAGE + NSTAGE * WCOLS
        VW = 2 * (P + 1)
        attn = work[:, 0:1024].rearrange("p (g n) -> p g n", g=2)
        k_pos = work[:, 1024:2048].rearrange("p (t n) -> p t n", t=TPB)
        v_sb = work[:, 2048:2048 + TPB * VW].rearrange("p (t n) -> p t n", t=TPB)
        KR = 2048 + TPB * VW
        k_relu = work[:, KR:KR + 512].rearrange("p (s n) -> p s n", s=2)
        QP = KR + 512
        q_pos = work[:, QP:QP + 1024].rearrange("p (m n) -> p m n", m=2)
        bias_raw = work[0:64, QP:QP + 768]
        q_relu = work[:, QP + 1024:QP + 1536]
        BH = QP + 1536
        bias16 = work[0:64, BH:BH + 384].bitcast(F16)
        assert BH + 384 <= WORK and STAGE + UNIT <= S4_AT and QP >= STAGE

        gate_ps = [pb("gate_ps0", [P, 512], F32), pb("gate_ps1", [P, 512], F32)]
        up_ps = [pb("up_ps0", [P, 512], F32), pb("up_ps1", [P, 512], F32)]
        wb_ps = pb("wb_ps", [P, 512], F32)
        y_ps = [pb("y_ps0", [P, 512], F32), pb("y_ps1", [P, 512], F32)]
        misc = pb("misc", [P, 512], F32)
        misc16 = misc[:, :].bitcast(F16)

        def y_tile(t):
            return y_ps[t // 2][:, (t % 2) * HID:(t % 2 + 1) * HID]

        ld_const = sem("ld_const")
        ld_x0 = sem("ld_x0")
        ld_x1 = sem("ld_x1")
        ld_x23 = sem("ld_x23")
        ld_sel = sem("ld_sel")
        ld_late = sem("ld_late")
        ld_att = sem("ld_att")
        ld_w = [sem(f"ld_w{i}") for i in range(NSTAGE)]
        w_hi_done = sem("w_hi_done")
        w_lo_done = sem("w_lo_done")
        ready = sem("ready")
        par_act = sem("par_act")
        par_pool = sem("par_pool")
        taps_done = sem("taps_done")
        stats = sem("stats")
        rstd_done = sem("rstd_done")
        xn_done = sem("xn_done")
        xT_ps = sem("xT_ps")
        xT_hi_done = sem("xT_hi_done")
        xT_lo_done = sem("xT_lo_done")
        logits_ps = sem("logits_ps")
        route_dve = [sem("route0_dve"), sem("route1_dve")]
        shifted = sem("shifted")
        expd = sem("expd")
        ws_done = sem("ws_done")
        wT_ps = sem("wT_ps")
        wT_done = sem("wT_done")
        gate_done = sem("gate_done")
        up_done = sem("up_done")
        wb_done = sem("wb_done")
        silu_done = sem("silu_done")
        p_done = sem("p_done")
        q_done = sem("q_done")
        h_hi_done = sem("h_hi_done")
        h_lo_done = sem("h_lo_done")
        down_done = sem("down_done")
        x_done = sem("x_done")
        y_tmp = sem("y_tmp")
        bias_ready0 = sem("bias_ready0")
        bias_ready = sem("bias_ready")
        kv_ps_done = sem("kv_ps_done")
        k_exp = sem("k_exp")
        k_done = sem("k_done")
        q_ps_done = sem("q_ps_done")
        q_exp = sem("q_exp")
        q_pos_done = sem("q_pos_done")
        sums_ps = sem("sums_ps")
        sums_done = sem("sums_done")
        ratio_ps = sem("ratio_ps")
        den_done = sem("den_done")
        den_inv = sem("den_inv")
        attn_done = sem("attn_done")
        o_ps_done = sem("o_ps_done")
        s4_ps_done = sem("s4_ps_done")
        w_ready = sem("w_ready")
        dve_init = sem("dve_init")
        waited = sem("waited")
        stored = sem("stored")

        block = ctx.enter_context(nc.Block())

        FFNS = [Ffn(0, C0, 0, 0, 0, True), Ffn(2, C0, 4 * C0, 4, 0, False),
                Ffn(3, C1, 8 * C0, 8, 1, False), Ffn(5, C1, 8 * C0 + 4 * C1, 12, 1, False)]
        ATT_PHASE, S4_PHASE = 1, 4
        SHAPE = {0: (4, 1, 3), 1: (2, 2, 2)}
        TCH, RCH = 4, 2
        for kind, chunks in ((0, C0), (1, C1)):
            ti, tp, ri = SHAPE[kind]
            assert ti * tp == TPB and 1 + ti * TCH + ri * RCH + 1 == chunks
        W_HI, W_LO = (w0_hi, w1_hi), (w0_lo, w1_lo)
        late_hi = w1_hi[:, :, :].rearrange("p c n -> p (c n)")
        late_lo = w1_lo[:, :, :].rearrange("p c n -> p (c n)")
        NEXP, NTOP = (E0, E1), (TOP0, TOP1)
        SEL0 = (0, C0 * P)
        BSEL = (C0 + C1) * P
        RT0 = (0, HC * E0)

        def nxt(b):
            return (b + 1) % NBLK if isinstance(b, int) else (b + 1) & (NBLK - 1)

        def odd(b):
            return b % 2 if isinstance(b, int) else b & 1

        def at(b):
            return b if isinstance(b, int) or b.max_val < NBLK else b & (NBLK - 1)

        def one(ap_index):
            return bass.ds(ap_index, 1)

        def unless_last(eng, b):
            return nullcontext() if isinstance(b, int) else eng.If(b < NBLK - 1)

        def each_block(eng, f, do):
            if f.late:
                do(0, True)
            with eng.Fori(1 if f.late else 0, NBLK) as b:
                do(b, False)

        def each_r(eng, f, splitting, do):
            ri = SHAPE[f.kind][2]
            with eng.Fori(0, ri - 1 if splitting else ri) as i:
                do(i, splitting)
            if splitting:
                do(ri - 1, False)

        LEAD = 3

        S = {}
        s_at = [0]

        def s4_array(name, n=16):
            S[name] = work[:, S4_AT + s_at[0]:S4_AT + s_at[0] + n]
            s_at[0] += n

        for nm in ("dt", "kc0", "kc1", "kc2", "kc3"):
            s4_array(nm, HC)
        for nm in ("are", "a", "ang0", "turn", "ang", "th", "sin", "sh", "em1", "ea", "cm1", "cos", "wre", "wim",
                   "ere", "t1", "t2", "inv", "fre", "fim", "cre", "cim", "nre", "nim", "aren", "omt"):
            s4_array(nm)
        s4_array("sum4", HC * 4)
        s4_array("diag", P)
        assert S4_AT + s_at[0] <= WORK
        PAR_A, PAR_T = 2, 10

        def pe_split3(pe, outs, lhs_hi, lhs_lo, rhs_hi, rhs_lo, start, stop, group=True):
            steps = ((lhs_hi, rhs_hi), (lhs_hi, rhs_lo), (lhs_lo, rhs_hi))
            for n, (a, c) in enumerate(steps):
                last = pe.matmul(outs, a, c, start=start and n == 0, stop=stop and n == 2,
                                 skip_group_check=not group)
            return last

        def pe_inner(pe, outs, f, b, c, col):
            hi, lo = W_HI[f.kind], W_LO[f.kind]
            for hc in range(HC):
                a = col + hc * P
                last = pe_split3(pe, outs, hi[:, one(c), a:a + P], lo[:, one(c), a:a + P],
                                 xT_hi[:, hc, one(at(b)), :], xT_lo[:, hc, one(at(b)), :],
                                 hc == 0, hc == HC - 1)
            return last

        def pe_gate_up(pe, f, b, c, par):
            k = f.k0 + b * f.chunks + c
            pe.wait_ge(silu_done, k + 1)
            pe_inner(pe, gate_ps[par][:, :], f, b, c, 0).then_inc(gate_done, 1)
            pe.wait_ge(p_done, k + 1)
            pe_inner(pe, up_ps[par][:, :], f, b, c, HC * P).then_inc(up_done, 1)

        def pe_spread(pe, f, b, c):
            k = f.k0 + b * f.chunks + c
            pe.wait_ge(q_done, k + 2)
            pe.matmul(wb_ps[:, :], sel[:, bass.ds(c * P + SEL0[f.kind], P)], wT[:, one(odd(b)), :],
                      start=True, stop=True).then_inc(wb_done, 1)

        def pe_down(pe, f, b, c, par, first=False, final=False):
            k = f.k0 + b * f.chunks + c
            hi, lo = W_HI[f.kind], W_LO[f.kind]
            w = 2 * HC * P
            if first:
                pe.wait_ge(x_done, 4 * f.phase + b + 4)
            pe.wait_ge(h_lo_done, k + 3)
            for t in range(TPB):
                last = pe_split3(pe, y_tile(t), h_hi[:, par, t * P:(t + 1) * P],
                                 h_lo[:, par, t * P:(t + 1) * P],
                                 hi[:, one(c), w:w + HID], lo[:, one(c), w:w + HID],
                                 first and t % 2 == 0, final, group=False)
            last.then_inc(down_done, 1)

        def pe_transposes(pe, blk, t, slot, routes):
            n = TPB * blk + t
            pe.wait_ge(xn_done, n + 1)
            if not (isinstance(n, int) and n == 0):
                pe.wait_ge(xT_lo_done, n)
            if not (isinstance(routes, int) and routes == 0):
                pe.wait_ge(wT_done, routes)
            for hc in range(HC):
                last = pe.transpose(misc[:, hc * P:(hc + 1) * P], xn[:, slot, hc * P:(hc + 1) * P],
                                    ident[:, :])
            last.then_inc(xT_ps, 1)

        def pe_logits(pe, f, b):
            r, e, o = f.r0 + b, NEXP[f.kind], RT0[f.kind]
            pe.wait_ge(xT_lo_done, TPB * (4 * f.phase + b + 1))
            if not (isinstance(r, int) and r == 0):
                pe.wait_ge(wT_done, r)
            for t in range(TPB):
                for hc in range(HC):
                    last = pe_split3(pe, misc[:, t * e:(t + 1) * e],
                                     xT_hi[:, hc, one(at(b)), t * P:(t + 1) * P],
                                     xT_lo[:, hc, one(at(b)), t * P:(t + 1) * P],
                                     rt_hi[:, o + hc * e:o + (hc + 1) * e],
                                     rt_lo[:, o + hc * e:o + (hc + 1) * e], hc == 0, hc == HC - 1)
            last.then_inc(logits_ps, 1)

        def pe_turn_weights(pe, f, b):
            pe.wait_ge(ws_done, f.r0 + b + 1)
            for t in range(TPB):
                last = pe.transpose(misc16[:, t * P:(t + 1) * P], ws[f.kind][:, t, :], ident16[:, :])
            last.then_inc(wT_ps, 1)

        def pe_ffn(pe, f):
            ti, tp, ri = SHAPE[f.kind]
            last_c = f.chunks - 1

            def slot(b, c, par, splitting):
                if splitting:
                    pe.wait_ge(w_lo_done, c + 2)
                pe_gate_up(pe, f, b, c + 1, 1 - par)
                pe_spread(pe, f, b, c + 1)
                pe_down(pe, f, b, c, par, first=isinstance(c, int) and c == 0)

            def do(b, splitting):
                nb = 4 * f.phase + b + 1
                slot(b, 0, 0, splitting)
                with pe.Fori(0, ti) as i:
                    for j in range(TCH):
                        if 1 <= j <= tp:
                            pe_transposes(pe, nb, i * tp + (j - 1), j - 1, f.r0 + b + 1)
                        slot(b, i * TCH + (1 + j), (1 + j) % 2, splitting)
                with unless_last(pe, b):
                    pe_logits(pe, f, b + 1)

                def r_iteration(i, splitting_r):
                    for j in range(RCH):
                        slot(b, i * RCH + (1 + ti * TCH + j), (1 + j) % 2, splitting)

                each_r(pe, f, splitting, r_iteration)
                with unless_last(pe, b):
                    pe_gate_up(pe, f, b + 1, 0, 0)
                    pe_turn_weights(pe, f, b + 1)
                pe_down(pe, f, b, last_c, 1, final=True)
                with unless_last(pe, b):
                    pe.wait_ge(wT_done, f.r0 + b + 2)
                    pe_spread(pe, f, b + 1, 0)

            if f.phase != ATT_PHASE + 1:
                pe_logits(pe, f, 0)
            if f.late:
                pe.wait_ge(w_lo_done, 1)
            pe_gate_up(pe, f, 0, 0, 0)
            pe_turn_weights(pe, f, 0)
            if f.late:
                pe.wait_ge(ld_sel, 16)
            pe.wait_ge(wT_done, f.r0 + 1)
            pe_spread(pe, f, 0, 0)
            each_block(pe, f, do)

        ATT = 4 * ATT_PHASE

        def pe_project_kv(pe, b):
            bank = (gate_ps[0], gate_ps[1])
            pe.wait_ge(xT_lo_done, TPB * (b + ATT + 1))
            for t in range(TPB):
                n = TPB * b + t
                if not (isinstance(n, int) and n < 2):
                    pe.wait_ge(k_exp, n - 1)
                pe.matmul(bank[t % 2][:, :], sel[0:64, BSEL:BSEL + P], bias16[:, 0:2 * HID],
                          start=True, stop=False)
                for hc in range(HC):
                    last = pe_split3(pe, bank[t % 2][:, :], xT_hi[:, hc, one(at(b)), t * P:(t + 1) * P],
                                     xT_lo[:, hc, one(at(b)), t * P:(t + 1) * P],
                                     w1_hi[:, C1 + hc, HID:3 * HID], w1_lo[:, C1 + hc, HID:3 * HID],
                                     False, hc == HC - 1)
                last.then_inc(kv_ps_done, 1)
                pe_transposes(pe, b + (ATT + 1), t, t % 2, 4)

        def pe_project_q(pe, b):
            for m in range(HC):
                if m == 0 and not isinstance(b, int):
                    pe.wait_ge(attn_done, 2 * b - 1)
                for hc in range(HC):
                    last = pe_split3(pe, up_ps[m][:, :], w1_hi[:, C1 + hc, m * P:(m + 1) * P],
                                     w1_lo[:, C1 + hc, m * P:(m + 1) * P],
                                     xT_hi[:, hc, one(at(b)), :], xT_lo[:, hc, one(at(b)), :],
                                     hc == 0, hc == HC - 1)
                last.then_inc(q_ps_done, 1)

        def pe_sums(pe, b):
            pe.wait_ge(k_done, TPB * b + TPB)
            for t in range(TPB):
                for g in range(2):
                    last = pe.matmul(wb_ps[:, g * (P + 1):(g + 1) * (P + 1)],
                                     k_pos[:, t, g * P:(g + 1) * P], v_sb[:, t, g * P:g * P + P + 1],
                                     start=t == 0 and g == 0, stop=t == TPB - 1, skip_group_check=True)
            last.then_inc(sums_ps, 1)

        def pe_ratios(pe, b):
            pe.wait_ge(q_pos_done, 2 * b + 2)
            pe.wait_ge(sums_done, b + 1)
            pe.wait_ge(x_done, b + ATT + 4)
            for g, (num, den) in enumerate(RATIO_BANKS):
                pe.matmul(den[:, :], ks_m[:, g, :], q_pos[:, g, :], start=True, stop=True)
                pe.matmul(num[:, :], kv_m[:, g, :], q_pos[:, g, :], start=True,
                          stop=True).then_inc(ratio_ps, 1)

        def pe_output(pe, b):
            pe.wait_ge(attn_done, 2 * b + 2)
            for t in range(TPB):
                pe.matmul(y_tile(t), sel[0:64, BSEL + P:BSEL + 2 * P], bias16[:, 2 * HID:3 * HID],
                          start=True, stop=False)
                for g in range(2):
                    last = pe.matmul(y_tile(t), attn[:, g, t * P:(t + 1) * P], o_w[:, g, :],
                                     start=False, stop=g == 1)
            last.then_inc(o_ps_done, 1)

        RATIO_BANKS = ((up_ps[1], up_ps[0]), (y_ps[0], wb_ps))

        def pe_attention(pe, f_next):
            pe.wait_ge(bias_ready, 1)
            pe_project_kv(pe, 0)
            pe_project_q(pe, 0)
            with pe.Fori(0, NBLK - 1) as b:
                pe_sums(pe, b)
                pe_project_kv(pe, b + 1)
                pe_ratios(pe, b)
                pe_project_q(pe, b + 1)
                pe_output(pe, b)
            last = NBLK - 1
            pe_sums(pe, last)
            pe_logits(pe, f_next, 0)
            pe_ratios(pe, last)
            pe_output(pe, last)

        def pe_s4(pe):
            base = 4 * S4_PHASE
            pe.wait_ge(taps_done, 1)
            for b in range(NBLK):
                pe.wait_ge(xT_lo_done, TPB * (b + base + 1))
                pe.wait_ge(x_done, b + base + 4)
                for t in range(TPB):
                    for hc in range(HC):
                        o = (t % 2) * HID + hc * P
                        for lag in range(b + 1):
                            last = pe_split3(pe, y_ps[t // 2][:, o:o + P],
                                             xT_hi[:, hc, b - lag, t * P:(t + 1) * P],
                                             xT_lo[:, hc, b - lag, t * P:(t + 1) * P],
                                             diag_hi[:, lag, hc, :], diag_lo[:, lag, hc, :],
                                             lag == 0, lag == b)
                last.then_inc(s4_ps_done, 1)
                for t in range(TPB):
                    pe_transposes(pe, base + b + 1, t, t % 2, 12)

        @block.tensor
        def _(pe):
            pe.wait_ge(ld_const, CONSTS)
            pe.wait_ge(ready, 1)
            for t in range(TPB):
                pe_transposes(pe, 0, t, t % 2, 0)
            pe_ffn(pe, FFNS[0])
            pe.wait_ge(w_lo_done, C0 + UNITS)
            pe_attention(pe, FFNS[1])
            pe_ffn(pe, FFNS[1])
            pe_ffn(pe, FFNS[2])
            pe_s4(pe)
            pe_ffn(pe, FFNS[3])

        def act_silu(a, f, b, c, par):
            k = f.k0 + b * f.chunks + c
            a.wait_ge(gate_done, k + 1)
            a.wait_ge(p_done, k + 1)
            a.activation(silu[:, par, :], gate_ps[par][:, :], ACT.Silu, scale=XW).then_inc(silu_done, 1)

        def act_h_hi(a, f, b, c, par):
            k = f.k0 + b * f.chunks + c
            a.wait_ge(q_done, k + 3)
            a.wait_ge(down_done, k + 1)
            a.activation(h_hi[:, par, :], qbuf[:, par, :], ACT.Copy).then_inc(h_hi_done, 1)

        def act_chunk(a, f, b, c, par):
            act_silu(a, f, b, c, par)
            act_h_hi(a, f, b, c, par)

        def act_xT_hi(a, blk, dst, t):
            n = TPB * blk + t
            a.wait_ge(xT_ps, n + 1)
            a.activation(xT_hi[:, :, one(dst), bass.ds(t * P, P)].rearrange("p h o n -> p h (o n)"),
                         misc[:, 0:HID].rearrange("p (h n) -> p h n", h=HC), ACT.Copy).then_inc(xT_hi_done, 1)

        def act_route_exp(a, f, b):
            a.wait_ge(shifted, f.r0 + b + 1)
            if f.kind == 0:
                a.activation(ex[:, :, :], wf[:, :, :], ACT.Exp).then_inc(expd, 1)
            else:
                a.activation(ex[:, :, 0:E1], lb[1][:, :, 0:E1], ACT.Exp, scale=-1.0).then_inc(expd, 1)

        def act_weights_T(a, f, b):
            a.wait_ge(wT_ps, f.r0 + b + 1)
            a.activation(wT[:, one(odd(b)), :], misc16[:, 0:BLK], ACT.Copy).then_inc(wT_done, 1)

        def act_weights_hi(a, n, s):
            a.wait_ge(ld_w[s], (n - s) * (16 // NSTAGE) + 16)
            a.activation(w0_hi[:, one(n), :], stage[:, s, :], ACT.Copy, scale=WS).then_inc(w_hi_done, 1)

        def act_late(a, n):
            a.wait_ge(ld_late, n * 16 + 16)
            a.activation(late_hi[:, bass.ds(n * UNIT, UNIT)], stage_late, ACT.Copy,
                         scale=WS).then_inc(w_hi_done, 1)

        def act_ffn(a, f):
            ti, tp, ri = SHAPE[f.kind]

            def do(b, splitting):
                nb = 4 * f.phase + b + 1
                act_chunk(a, f, b, 1, 1)
                if splitting:
                    act_weights_hi(a, LEAD, LEAD % 2)
                with a.Fori(0, ti) as i:
                    for j in range(TCH):
                        c = i * TCH + (1 + j)
                        if 2 <= j <= tp + 1:
                            act_xT_hi(a, nb, nxt(b), i * tp + (j - 2))
                        act_chunk(a, f, b, c + 1, j % 2)
                        if splitting:
                            act_weights_hi(a, c + LEAD, (1 + j + LEAD) % 2)
                    if f.late and not splitting:
                        act_late(a, b * ti + i - ti)
                with unless_last(a, b):
                    act_route_exp(a, f, b + 1)

                def r_iteration(i, splitting_r):
                    for j in range(RCH):
                        c = i * RCH + (1 + ti * TCH + j)
                        act_chunk(a, f, b, c + 1, j % 2)
                        if splitting_r:
                            act_weights_hi(a, c + LEAD, (1 + j + LEAD) % 2)

                each_r(a, f, splitting, r_iteration)
                with unless_last(a, b):
                    act_silu(a, f, b + 1, 0, 0)
                    act_weights_T(a, f, b + 1)
                    act_h_hi(a, f, b + 1, 0, 0)

            if f.late:
                act_weights_hi(a, 0, 0)
                act_weights_hi(a, 1, 1)
            if f.phase != ATT_PHASE + 1:
                act_route_exp(a, f, 0)
            if f.late:
                act_weights_hi(a, 2, 0)
            act_silu(a, f, 0, 0, 0)
            act_weights_T(a, f, 0)
            act_h_hi(a, f, 0, 0, 0)
            each_block(a, f, do)

        def act_project_kv(a, b):
            for t in range(TPB):
                n = TPB * b + t
                a.wait_ge(kv_ps_done, n + 1)
                if not (isinstance(b, int) and b == 0):
                    a.wait_ge(sums_ps, b)
                bank = gate_ps[t % 2]
                a.activation(k_pos[:, t, :], bank[:, 0:HID], ACT.Exp, scale=XW)
                if not (isinstance(n, int) and n < 2):
                    a.wait_ge(k_done, n - 1)
                a.activation(k_relu[:, t % 2, :], bank[:, 0:HID], ACT.Relu, scale=XW)
                a.activation(v_sb[:, t, :].rearrange("p (g n) -> p g n", g=2)[:, :, 0:P],
                             bank[:, HID:2 * HID].rearrange("p (g n) -> p g n", g=2), ACT.Copy,
                             scale=XW).then_inc(k_exp, 1)
                act_xT_hi(a, b + (ATT + 1), nxt(b), t)

        def act_project_q(a, b):
            for m in range(HC):
                bias = small[:, PQB + m:PQB + m + 1]
                a.wait_ge(q_ps_done, 2 * b + m + 1)
                a.activation(q_pos[:, m, :], up_ps[m][:, :], ACT.Exp, scale=XW, bias=bias)
                if not (isinstance(b, int) and b + m == 0):
                    a.wait_ge(q_pos_done, 2 * b + m)
                a.activation(q_relu, up_ps[m][:, :], ACT.Relu, scale=XW, bias=bias).then_inc(q_exp, 1)

        def act_ratios(a, b):
            for g, (num, den) in enumerate(RATIO_BANKS):
                a.wait_ge(ratio_ps, 2 * b + g + 1)
                a.wait_ge(o_ps_done, b + 1)
                a.activation(attn[:, g, :], den[:, :], ACT.Identity, bias=eps_t[:, :]).then_inc(den_done, 1)

        def act_attention(a, f_next):
            act_project_kv(a, 0)
            act_project_q(a, 0)
            with a.Fori(0, NBLK - 1) as b:
                act_project_kv(a, b + 1)
                act_ratios(a, b)
                act_project_q(a, b + 1)
            act_route_exp(a, f_next, 0)
            act_ratios(a, NBLK - 1)

        def act_s4(a):
            base = 4 * S4_PHASE
            with a.Fori(0, NBLK) as b:
                for t in range(TPB):
                    act_xT_hi(a, b + base + 1, nxt(b), t)

        @block.scalar
        def _(a):
            for s in (silu_done, h_hi_done):
                a.sem_inc(s, 2)
            a.sem_inc(o_ps_done, 1)
            a.wait_ge(ld_const, CONSTS)
            a.activation(S["dt"], small[:, PDT:PDT + HC], ACT.Exp).then_inc(par_act, 1)
            a.activation(S["are"], small[:, PAR:PAR + 16], ACT.Exp).then_inc(par_act, 1)
            a.wait_ge(par_pool, PAR_A)
            a.activation(S["th"], S["a"], ACT.Tanh, scale=0.5).then_inc(par_act, 1)
            a.wait_ge(par_pool, PAR_T)
            a.activation(S["sin"], S["ang"], ACT.Sin).then_inc(par_act, 1)
            a.activation(S["sh"], S["ang"], ACT.Sin, scale=0.5).then_inc(par_act, 1)
            for t in range(TPB):
                act_xT_hi(a, 0, 0, t)
            act_ffn(a, FFNS[0])
            act_attention(a, FFNS[1])
            act_ffn(a, FFNS[1])
            act_ffn(a, FFNS[2])
            act_s4(a)
            act_ffn(a, FFNS[3])

        class Chain:

            def __init__(self, eng, s, base):
                self.eng, self.s, self.n = eng, s, base

            def step(self, ins):
                ins.then_inc(self.s, 1)
                self.n = self.n + 1

            def then(self, ins):
                self.step(ins)
                self.eng.wait_ge(self.s, self.n)

            def then_alone(self, ins):
                self.then(ins)
                self.eng.sem_inc(waited, 1)

        def dve_stats(v, blk, src):
            ch = Chain(v, stats, blk * 3)
            if not (isinstance(blk, int) and blk == 0):
                v.wait_ge(x_done, blk + 1)
            for t in range(TPB):
                ins = v.bn_stats(bn[:, t, :], x[:, one(src * TPB + t), :])
            ch.then_alone(ins)
            for t in range(TPB):
                ins = v.bn_aggr(mv[:, t, :], bn[:, t, :])
            ch.then(ins)
            ch.step(v.tensor_scalar(ve[:, :], mv[:, :, 1], EPS, 1.0 / (XS * XS), ALU.add, ALU.mult))

        def dve_normalise(v, blk, src, t, slot, slots=2):
            n = TPB * blk + t
            v.wait_ge(rstd_done, blk + 1)
            if not (isinstance(n, int) and n < slots):
                v.wait_ge(xT_ps, n + (1 - slots))
            v.tensor_scalar(xn[:, slot, :], x[:, one(src * TPB + t), :], mv[:, one(t), 0:1],
                            rstd[:, one(t)], ALU.subtract, ALU.mult).then_inc(xn_done, 1)

        def dve_xT_lo(v, blk, dst, t):
            n = TPB * blk + t
            v.wait_ge(xT_hi_done, n + 1)
            sl = (slice(None), slice(None), one(dst), bass.ds(t * P, P))
            v.tensor_tensor(xT_lo[sl].rearrange("p h o n -> p h (o n)"),
                            misc[:, 0:HID].rearrange("p (h n) -> p h n", h=HC),
                            xT_hi[sl].rearrange("p h o n -> p h (o n)"),
                            ALU.subtract).then_inc(xT_lo_done, 1)

        def dve_tiles(v, blk, src):
            dve_normalise(v, blk, src, 0, 0)
            for t in range(TPB):
                if t + 1 < TPB:
                    dve_normalise(v, blk, src, t + 1, (t + 1) % 2)
                dve_xT_lo(v, blk, src, t)

        def route_steps(kind):
            return 7 if kind == 0 else 9

        def dve_route_choose(v, f, b):
            e, k, kind = NEXP[f.kind], NTOP[f.kind], f.kind
            rl = b + (4 if f.phase in (2, 5) else 0)
            ch = Chain(v, route_dve[kind], rl * route_steps(kind))
            v.wait_ge(logits_ps, f.r0 + b + 1)
            ch.then_alone(v.tensor_scalar(lb[kind][:, :, 0:e], misc[:, 0:TPB * e].rearrange("p (t e) -> p t e", t=TPB),
                                    XW, None, ALU.mult))
            for t in range(TPB):
                ins = v.max(m8[:, t, :], lb[kind][:, t, 0:e])
            ch.then(ins)
            if kind == 0:
                v.tensor_tensor(wf[:, :, :], lb[0][:, :, 0:e],
                                m8[:, :, 0:1].to_broadcast([P, TPB, e]), ALU.subtract).then_inc(shifted, 1)
            else:
                v.tensor_scalar(m8[:, :, 6:8], m8[:, :, 6:8], 1.0, None, ALU.mult).then_inc(shifted, 1)
            ch.then_alone(v.tensor_copy(top[kind][:, :, 0:k], m8[:, :, 0:k]))
            for t in range(TPB):
                ins = v.match_replace(rb[kind][:, t, :], top[kind][:, t, :], lb[kind][:, t, :], TAKEN)
            ch.step(ins)

        def dve_route_weigh(v, f, b):
            e, kind = NEXP[f.kind], f.kind
            rl = b + (4 if f.phase in (2, 5) else 0)
            ch = Chain(v, route_dve[kind], rl * route_steps(kind) + 4)
            v.wait_ge(route_dve[kind], ch.n)
            v.wait_ge(expd, f.r0 + b + 1)
            prob = ex[:, :, 0:e]
            if kind == 1:
                ch.then(v.tensor_scalar(prob, prob, 1.0, None, ALU.add))
                ch.then(v.reciprocal(prob, prob))
            w = wf[:, :, 0:e]
            ch.then(v.scalar_tensor_tensor(w, rb[kind][:, :, 0:e], TAKEN, prob, ALU.is_equal, ALU.mult))
            ch.then(v.tensor_reduce(rsum[:, :], w, AXX, ALU.add))
            if kind == 1:
                v.tensor_scalar(rsum[:, :], rsum[:, :], 1e-20, None, ALU.add).then_inc(y_tmp, 1)
                v.wait_ge(y_tmp, rl + 1)
            ch.then(v.reciprocal(rrec[:, :], rsum[:, :]))
            scale = RS * HALF * (1.0 if kind == 0 else ROUTE1_SCALE)
            if not (isinstance(b, int) and f.r0 + b == 0):
                v.wait_ge(wT_ps, f.r0 + b)
            v.tensor_tensor(w, w, rrec[:, :].unsqueeze(2).to_broadcast([P, TPB, e]), ALU.mult).then_inc(
                w_ready, 1)
            v.wait_ge(w_ready, 2 * (f.r0 + b) + 1)
            v.tensor_scalar(ws[kind][:, :, 0:e], w, scale, None, ALU.mult).then_inc(w_ready, 1)
            v.wait_ge(w_ready, 2 * (f.r0 + b) + 2)
            v.scalar_tensor_tensor(ws[kind][:, :, LO_ROW:LO_ROW + e], w, scale, ws[kind][:, :, 0:e],
                                   ALU.mult, ALU.subtract).then_inc(ws_done, 1)


        def dve_chunk(v, f, b, c, par):
            k = f.k0 + b * f.chunks + c
            v.wait_ge(silu_done, k + 3)
            v.wait_ge(up_done, k + 1)
            v.scalar_tensor_tensor(pbuf, up_ps[par][:, :], P_SCALE, silu[:, par, :], ALU.mult,
                                   ALU.mult).then_inc(p_done, 1)
            v.wait_ge(p_done, k + 3)
            v.wait_ge(wb_done, k + 1)
            v.wait_ge(h_hi_done, k + 1)
            v.tensor_tensor(qbuf[:, par, :], pbuf, wb_ps[:, :], ALU.mult).then_inc(q_done, 1)
            v.wait_ge(h_hi_done, k + 3)
            v.tensor_tensor(h_lo[:, par, :], qbuf[:, par, :], h_hi[:, par, :],
                            ALU.subtract).then_inc(h_lo_done, 1)

        def dve_add_y(v, phase, b, scale):
            for m in range(2):
                xs = x[:, bass.ds(b * TPB + 2 * m, 2), :].rearrange("p t n -> p (t n)")
                ins = v.scalar_tensor_tensor(xs, y_ps[m][:, :], scale, xs, ALU.mult, ALU.add)
            ins.then_inc(x_done, 1)

        def dve_weights_lo(v, n, s):
            v.wait_ge(w_hi_done, n + 1)
            v.scalar_tensor_tensor(w0_lo[:, one(n), :], stage[:, s, :], WS, w0_hi[:, one(n), :],
                                   ALU.mult, ALU.subtract).then_inc(w_lo_done, 1)

        def dve_late(v, n):
            v.wait_ge(w_hi_done, n + (C0 + 1))
            at_n = bass.ds(n * UNIT, UNIT)
            v.scalar_tensor_tensor(late_lo[:, at_n], stage_late, WS, late_hi[:, at_n],
                                   ALU.mult, ALU.subtract).then_inc(w_lo_done, 1)

        def dve_ffn(v, f):
            ti, tp, ri = SHAPE[f.kind]

            def do(b, splitting):
                nb = 4 * f.phase + b + 1
                if f.late:
                    v.wait_ge(ld_x1 if splitting else ld_x23, 16)
                dve_stats(v, nb, nxt(b))
                dve_chunk(v, f, b, 1, 1)
                if splitting:
                    dve_weights_lo(v, LEAD, LEAD % 2)
                with v.Fori(0, ti) as i:
                    for j in range(TCH):
                        c = i * TCH + (1 + j)
                        if j < tp:
                            dve_normalise(v, nb, nxt(b), i * tp + j, j, tp)
                        if 2 <= j <= tp + 1:
                            dve_xT_lo(v, nb, nxt(b), i * tp + (j - 2))
                        dve_chunk(v, f, b, c + 1, j % 2)
                        if splitting:
                            dve_weights_lo(v, c + LEAD, (1 + j + LEAD) % 2)
                    if f.late and not splitting:
                        dve_late(v, b * ti + i - ti)
                with unless_last(v, b):
                    dve_route_choose(v, f, b + 1)

                def r_iteration(i, splitting_r):
                    for j in range(RCH):
                        c = i * RCH + (1 + ti * TCH + j)
                        dve_chunk(v, f, b, c + 1, j % 2)
                        if splitting_r:
                            dve_weights_lo(v, c + LEAD, (1 + j + LEAD) % 2)

                each_r(v, f, splitting, r_iteration)
                with unless_last(v, b):
                    dve_route_weigh(v, f, b + 1)
                    dve_chunk(v, f, b + 1, 0, 0)
                v.wait_ge(down_done, f.k0 + b * f.chunks + (f.chunks + 2))
                dve_add_y(v, f.phase, b, 1.0 / (HS * WS))

            if f.late:
                dve_weights_lo(v, 0, 0)
                dve_weights_lo(v, 1, 1)
            if f.phase != ATT_PHASE + 1:
                dve_route_choose(v, f, 0)
            if f.late:
                dve_weights_lo(v, 2, 0)
            if f.phase != ATT_PHASE + 1:
                dve_route_weigh(v, f, 0)
            dve_chunk(v, f, 0, 0, 0)
            each_block(v, f, do)

        def dve_project_kv(v, b):
            blk = b + (ATT + 1)
            for t in range(2):
                dve_normalise(v, blk, nxt(b), t, t)
            for t in range(TPB):
                n = TPB * b + t
                v.wait_ge(k_exp, n + 1)
                v.scalar_tensor_tensor(k_pos[:, t, :], k_pos[:, t, :], 1.0, k_relu[:, t % 2, :],
                                       ALU.min, ALU.add).then_inc(k_done, 1)
                dve_xT_lo(v, blk, nxt(b), t)
                if t + 2 < TPB:
                    dve_normalise(v, blk, nxt(b), t + 2, t % 2)

        def dve_project_q(v, b):
            for m in range(HC):
                v.wait_ge(q_exp, 2 * b + m + 1)
                v.scalar_tensor_tensor(q_pos[:, m, :], q_pos[:, m, :], 1.0, q_relu, ALU.min,
                                       ALU.add).then_inc(q_pos_done, 1)

        def dve_sums(v, b):
            v.wait_ge(sums_ps, b + 1)
            w = P + 1
            v.tensor_tensor(kv_m[:, 0, :], wb_ps[:, 0:P], mask[:, :], ALU.mult)
            v.tensor_scalar(ks_m[:, 0, :], mask[:, :], wb_ps[:, P:w], None, ALU.mult)
            v.tensor_tensor(kv_m[:, 1, :], wb_ps[:, w + 1:2 * w], mask[:, :], ALU.mult)
            v.tensor_scalar(ks_m[:, 1, :], mask[:, :], wb_ps[:, w:w + 1], None,
                            ALU.mult).then_inc(sums_done, 1)

        def dve_ratios(v, b):
            for g, (num, den) in enumerate(RATIO_BANKS):
                v.wait_ge(den_done, 2 * b + g + 1)
                v.reciprocal(attn[:, g, :], attn[:, g, :]).then_inc(den_inv, 1)
                v.wait_ge(den_inv, 2 * b + g + 1)
                v.tensor_tensor(attn[:, g, :], num[:, :], attn[:, g, :], ALU.mult).then_inc(attn_done, 1)

        def dve_output(v, b):
            v.wait_ge(o_ps_done, b + 2)
            dve_add_y(v, ATT_PHASE, b, 1.0)

        def dve_attention(v, f_next):
            v.wait_ge(ld_att, 48)
            v.wait_ge(taps_done, 1)
            v.tensor_copy(bias16[:, :], bias_raw).then_inc(bias_ready0, 1)
            v.wait_ge(bias_ready0, 1)
            v.tensor_tensor(bias16[LO_ROW:2 * LO_ROW, :], bias_raw[LO_ROW:2 * LO_ROW, :],
                            bias16[LO_ROW:2 * LO_ROW, :], ALU.subtract)
            for t in range(TPB):
                ins = v.memset(v_sb[:, t, P:P + 1], 1.0)
            ins.then_inc(bias_ready, 1)
            dve_stats(v, ATT + 1, 1)
            dve_project_kv(v, 0)
            dve_project_q(v, 0)
            with v.Fori(0, NBLK - 1) as b:
                dve_stats(v, b + (ATT + 2), nxt(b + 1))
                dve_sums(v, b)
                dve_project_kv(v, b + 1)
                dve_ratios(v, b)
                dve_project_q(v, b + 1)
                dve_output(v, b)
            last = NBLK - 1
            dve_sums(v, last)
            dve_route_choose(v, f_next, 0)
            dve_ratios(v, last)
            dve_route_weigh(v, f_next, 0)
            dve_output(v, last)

        def dve_s4(v):
            base = 4 * S4_PHASE
            with v.Fori(0, NBLK) as b:
                dve_stats_after = b + base + 1
                v.wait_ge(s4_ps_done, b + 1)
                dve_add_y(v, S4_PHASE, b, XW)
                dve_stats(v, dve_stats_after, nxt(b))
                dve_tiles(v, dve_stats_after, nxt(b))

        @block.vector
        def _(v):
            for s in (p_done, q_done, h_lo_done):
                v.sem_inc(s, 2)
            v.sem_inc(down_done, 2)
            ch = Chain(v, dve_init, 0)
            for s in range(2):
                ch.step(v.memset(ws[s][:, :, :].bitcast(F32), 0.0))
            ch.step(v.memset(sel[64:P, :].bitcast(F32), 0.0))
            ch.step(v.memset(mhalf[:, :], -0.5))
            v.memset(eps_t[:, :], ATT_EPS)
            for s, (e, k) in enumerate(((E0, TOP0), (E1, TOP1))):
                ch.step(v.memset(lb[s][:, :, e:e + 8 - k], NEVER))
                ch.step(v.memset(top[s][:, :, k:8], NEVER))
            v.wait_ge(dve_init, ch.n)
            ch.step(v.memset(ws[1][:, :, E1:R1], RS * HALF))
            v.wait_ge(ld_const, CONSTS)
            ch.step(v.tensor_copy(ident16[:, :], ident[:, :]))
            ch.then(v.tensor_scalar(rt_hi[:, :], small[:, PR0:PCOLS], WS, None, ALU.mult))
            ch.then(v.scalar_tensor_tensor(rt_lo[:, :], small[:, PR0:PCOLS], WS, rt_hi[:, :], ALU.mult,
                                           ALU.subtract))
            v.sem_inc(ready, 1)
            v.wait_ge(ld_x0, 16)
            dve_stats(v, 0, 0)
            dve_tiles(v, 0, 0)
            v.sem_inc(x_done, NBLK)
            dve_ffn(v, FFNS[0])
            dve_attention(v, FFNS[1])
            dve_ffn(v, FFNS[1])
            dve_ffn(v, FFNS[2])
            dve_s4(v)
            dve_ffn(v, FFNS[3])


        def pool_s4_angles(v):
            ch = Chain(v, par_pool, 0)
            tt = v.tensor_tensor
            v.wait_ge(par_act, 2)
            dtb = S["dt"].unsqueeze(2).to_broadcast([P, HC, NS4])
            ch.then(v.tensor_scalar(S["aren"], S["are"], -1.0, None, ALU.mult))
            ch.then(tt(per_state(S["a"]), per_state(S["aren"]), dtb, ALU.mult))
            assert ch.n == PAR_A
            ch.then(tt(per_state(S["ang0"]), per_state(small[:, PAI:PAI + 16]), dtb, ALU.mult))
            magic = 12582912.0
            ch.then(v.tensor_scalar(S["turn"], S["ang0"], 1.0 / (2 * np.pi), magic, ALU.mult, ALU.add))
            ch.then(v.tensor_scalar(S["turn"], S["turn"], magic, None, ALU.subtract))
            c1 = 6.28125
            c2 = 2 * np.pi - c1
            for part in (c1, c2):
                ch.then(v.tensor_scalar(S["t1"], S["turn"], part, None, ALU.mult))
                ch.then(tt(S["ang0"], S["ang0"], S["t1"], ALU.subtract))
            ch.then(v.tensor_scalar(S["ang"], S["ang0"], 3.1415925, -3.1415925, ALU.min, ALU.max))
            assert ch.n == PAR_T

        def per_state(ap):
            return ap.rearrange("p (h n) -> p h n", h=HC)

        def pool_s4_taps(v):
            ch = Chain(v, par_pool, PAR_T)
            tt = v.tensor_tensor
            ai = small[:, PAI:PAI + 16]

            def inverse(ap):
                ch.then(tt(ap, ap, minus1[:, :], ALU.pow))

            v.wait_ge(par_act, 5)
            ch.then(v.tensor_scalar(S["omt"], S["th"], -1.0, 1.0, ALU.mult, ALU.add))
            inverse(S["omt"])
            ch.then(v.tensor_scalar(S["t1"], S["th"], 2.0, None, ALU.mult))
            ch.then(tt(S["em1"], S["t1"], S["omt"], ALU.mult))
            ch.then(v.tensor_scalar(S["ea"], S["em1"], 1.0, None, ALU.add))
            ch.then(v.tensor_scalar(S["t1"], S["sh"], -2.0, None, ALU.mult))
            ch.then(tt(S["cm1"], S["t1"], S["sh"], ALU.mult))
            ch.then(v.tensor_scalar(S["cos"], S["cm1"], 1.0, None, ALU.add))
            ch.then(tt(S["wre"], S["ea"], S["cos"], ALU.mult))
            ch.then(tt(S["wim"], S["ea"], S["sin"], ALU.mult))
            ch.then(tt(S["t1"], S["em1"], S["cos"], ALU.mult))
            ch.then(tt(S["ere"], S["t1"], S["cm1"], ALU.add))

            def product(re, im, are, aim, bre, bim):
                ch.then(tt(S["t1"], aim, bim, ALU.mult))
                ch.then(tt(S["t2"], are, bre, ALU.mult))
                ch.then(tt(re, S["t2"], S["t1"], ALU.subtract))
                ch.then(tt(S["t1"], are, bim, ALU.mult))
                ch.then(tt(S["t2"], aim, bre, ALU.mult))
                ch.then(tt(im, S["t2"], S["t1"], ALU.add))

            ch.then(tt(S["t1"], S["aren"], S["aren"], ALU.mult))
            ch.then(tt(S["t2"], ai, ai, ALU.mult))
            ch.then(tt(S["inv"], S["t1"], S["t2"], ALU.add))
            inverse(S["inv"])
            ch.then(v.tensor_scalar(S["nim"], ai, -1.0, None, ALU.mult))
            product(S["fre"], S["fim"], S["ere"], S["wim"], S["aren"], S["nim"])
            ch.then(tt(S["fre"], S["fre"], S["inv"], ALU.mult))
            ch.then(tt(S["fim"], S["fim"], S["inv"], ALU.mult))
            product(S["cre"], S["cim"], small[:, PCR:PCR + 16], small[:, PCI:PCI + 16], S["fre"], S["fim"])
            for lag in range(NBLK):
                kc = S[f"kc{lag}"]
                terms, halves = per_state(S["cre"]), S["sum4"].rearrange("p (h n) -> p h n", h=HC)
                ch.then(tt(halves[:, :, 0:4], terms[:, :, 0:4], terms[:, :, 4:8], ALU.add))
                ch.then(tt(halves[:, :, 0:2], halves[:, :, 0:2], halves[:, :, 2:4], ALU.add))
                ch.then(tt(kc.unsqueeze(2), halves[:, :, 0:1], halves[:, :, 1:2], ALU.add))
                ch.then(v.tensor_scalar(kc, kc, 2.0 * WS, None, ALU.mult))
                if lag == 0:
                    ch.then(v.tensor_scalar(S["t1"][:, 0:HC], small[:, PD:PD + HC], WS, None, ALU.mult))
                    ch.then(tt(kc, kc, S["t1"][:, 0:HC], ALU.add))
                for hc in range(HC):
                    ch.then(v.tensor_scalar(S["diag"], ident[:, :], kc[:, hc:hc + 1], None, ALU.mult))
                    ch.then(v.tensor_copy(diag_hi[:, lag, hc, :], S["diag"]))
                    ch.then(tt(diag_lo[:, lag, hc, :], S["diag"], diag_hi[:, lag, hc, :], ALU.subtract))
                if lag < NBLK - 1:
                    product(S["nre"], S["nim"], S["cre"], S["cim"], S["wre"], S["wim"])
                    ch.then(v.tensor_copy(S["cre"], S["nre"]))
                    ch.then(v.tensor_copy(S["cim"], S["nim"]))
            v.sem_inc(taps_done, 1)

        @block.gpsimd
        def _(pool):
            def rsqrt(blk):
                pool.wait_ge(stats, 3 * blk + 3)
                pool.tensor_tensor(rstd[:, :], ve[:, :], mhalf[:, :], ALU.pow).then_inc(rstd_done, 1)

            pool.memset(minus1[:, :], -1.0)
            pool.wait_ge(ld_const, CONSTS)
            pool_s4_angles(pool)
            pool.wait_ge(dve_init, 8)
            rsqrt(0)
            rsqrt(1)
            pool_s4_taps(pool)
            with pool.Fori(2, NBLK * 6 + 1) as i:
                rsqrt(i)

        @block.sync
        def _(sp):
            sp.dma_start(small[:, :], small_in).then_inc(ld_const, 16)
            sp.dma_start(x[:, 0:TPB, :], x_in[:, 0:TPB, :]).then_inc(ld_x0, 16)
            sp.dma_start(ident[:, :], ident_in).then_inc(ld_const, 16)
            for s in range(NSTAGE):
                sp.dma_start(stage[:, s, :], w0_in[s]).then_inc(ld_w[s], 16)
            sp.dma_start(sel[0:64, :], sel_in).then_inc(ld_sel, 16)
            sp.dma_start(x[:, TPB:2 * TPB, :], x_in[:, TPB:2 * TPB, :]).then_inc(ld_x1, 16)
            with sp.Fori(1, C0 // NSTAGE) as i:
                for s in range(NSTAGE):
                    n = i * NSTAGE + s
                    sp.wait_ge(w_lo_done, n + (1 - NSTAGE))
                    sp.dma_start(stage[:, s, :], w0_in[one(n)].rearrange("o p n -> (o p) n")).then_inc(
                        ld_w[s], 16)
            sp.dma_start(x[:, 2 * TPB:, :], x_in[:, 2 * TPB:, :]).then_inc(ld_x23, 16)
            sp.dma_start(o_w[:, :, :], ow_in).then_inc(ld_att, 16)
            sp.dma_start(mask[:, :], mask_in).then_inc(ld_att, 16)
            with sp.Fori(0, UNITS) as n:
                sp.wait_ge(w_lo_done, n + C0)
                sp.dma_start(stage_late, late_in[one(n)].rearrange("o p n -> (o p) n")).then_inc(
                    ld_late, 16)
            sp.wait_ge(w_lo_done, C0 + UNITS)
            sp.dma_start(bias_raw, bias_in.to_broadcast([64, 768])).then_inc(ld_att, 16)
            base = 4 * 5 + 4
            with sp.Fori(0, NBLK) as b:
                sp.wait_ge(x_done, b + base + 1)
                sp.dma_start(out[:, bass.ds(b * TPB, TPB), :], x[:, bass.ds(b * TPB, TPB), :]).then_inc(
                    stored, 16)
            sp.wait_ge(stored, 16 * NBLK)


CONSTS = 32


def kernel(**inputs):
    import numpy as _np
    import concourse.bacc as _bacc
    from concourse import mybir as _mybir
    from concourse.bass_utils import run_bass_kernel_spmd as _run

    f32 = _np.float32
    a = {k: _np.asarray(v) for k, v in inputs.items()}

    def chunks_of_rows(w, n):
        pad = _np.zeros((n * P - w.shape[0], w.shape[1]), w.dtype)
        w = _np.concatenate([w, pad], 0).reshape(n, P, HC, P)
        return w.transpose(0, 3, 2, 1).reshape(n, P, HC * P)

    def chunks_of_down(w, n):
        pad = _np.zeros((n * P - w.shape[0], w.shape[1]), w.dtype)
        return _np.concatenate([w, pad], 0).reshape(n, P, HID)

    def rows(w):
        return w.reshape(-1, w.shape[-1])

    w0 = _np.concatenate([
        chunks_of_rows(rows(a["L0_ffn_gate_w"]), C0), chunks_of_rows(rows(a["L0_ffn_up_w"]), C0),
        chunks_of_down(rows(a["L0_ffn_down_w"].transpose(0, 2, 1)), C0)], 2)
    gate1 = _np.concatenate([rows(a["L1_ffn_exp_wg"]), a["L1_ffn_shared_wg"]], 0)
    up1 = _np.concatenate([rows(a["L1_ffn_exp_wu"]), a["L1_ffn_shared_wu"]], 0)
    down1 = _np.concatenate([rows(a["L1_ffn_exp_wd"].transpose(0, 2, 1)), a["L1_ffn_shared_wd"].T], 0)
    w1 = _np.concatenate([chunks_of_rows(gate1, C1), chunks_of_rows(up1, C1), chunks_of_down(down1, C1)], 2)
    qkv = _np.concatenate([a["L0_attn_q_w"].T, a["L0_attn_k_w"].T, a["L0_attn_v_w"].T], 1).reshape(HC, P, 3 * HID)
    late = _np.concatenate([w1, qkv], 0).transpose(1, 0, 2).reshape(P, UNITS, UNIT).transpose(1, 0, 2)

    def halves(v):
        v = v.reshape(HC, P, -1)
        return v.transpose(1, 0, 2).reshape(P, -1)

    small = _np.concatenate([
        halves(a["L0_attn_q_b"]), halves(a["L1_attn_log_dt"]), halves(a["L1_attn_D_param"]),
        halves(a["L1_attn_A_real_log"]), halves(a["L1_attn_A_imag"]), halves(a["L1_attn_C_re"]),
        halves(a["L1_attn_C_im"]), halves(a["L0_ffn_router_w"].T), halves(a["L1_ffn_gate_w"].T)], 1)
    bias = _np.concatenate([a["L0_attn_k_b"], a["L0_attn_v_b"], a["L0_attn_o_b"]]).reshape(1, 3 * HID)
    ow = a["L0_attn_o_w"].T.reshape(HC, P, HID).transpose(1, 0, 2)
    ident = _np.eye(P, dtype=f32)
    mask = _np.kron(_np.eye(P // HD), _np.ones((HD, HD))).astype(f32)
    sel = _np.zeros((64, (C0 + C1 + 2) * P), _np.float16)
    for n, scale in enumerate((XS * WS, 1.0)):
        o = (C0 + C1 + n) * P
        sel[0, o:o + P] = sel[LO_ROW, o:o + P] = scale
    for e in range(E0):
        sel[e, e * I0:(e + 1) * I0] = sel[LO_ROW + e, e * I0:(e + 1) * I0] = 1
    for e in range(R1):
        o = C0 * P + e * I1
        sel[e, o:o + I1] = sel[LO_ROW + e, o:o + I1] = 1
    xin = a["L0_attn_hidden_states"].reshape(NBLK * TPB, P, HID).transpose(1, 0, 2)

    given = dict(x=xin, w0=w0, late=late, small=small, bias=bias, ow=ow, sel=sel, ident=ident, mask=mask)
    nc = _bacc.Bacc("TRN2", target_bir_lowering=False, num_devices=1)
    arrays = {f"{n}_dram": _np.ascontiguousarray(v) for n, v in given.items()}
    d = {n: nc.dram_tensor(f"{n}_dram", arrays[f"{n}_dram"].shape,
                           _mybir.dt.from_np(arrays[f"{n}_dram"].dtype), kind="ExternalInput").ap()
         for n in given}
    out = nc.dram_tensor("out_0_dram", (P, NBLK * TPB, HID), F32, kind="ExternalOutput").ap()
    build(nc, d["x"], d["w0"], d["late"], d["small"], d["bias"], d["ow"], d["sel"], d["ident"],
          d["mask"], out)
    r = _run(nc, [arrays], core_ids=[0])
    return r.results[0]["out_0_dram"].transpose(1, 0, 2).reshape(NBLK, BLK, HID)
```

```python
from contextlib import ExitStack, nullcontext
from collections import namedtuple

import numpy as np
import concourse.bass as bass
from concourse import mybir

F32 = mybir.dt.float32
F16 = mybir.dt.float16
ALU = mybir.AluOpType
ACT = mybir.ActivationFunctionType
AXX = mybir.AxisListType.X

P = 128
HID = 256
HC = HID // P
NBLK = 4
BLK = 512
TPB = BLK // P
E0, I0, TOP0 = 32, 96, 4
E1, I1, TOP1, SHARED1 = 8, 176, 2, 352
C0 = E0 * I0 // P
C1 = -(-(E1 * I1 + SHARED1) // P)
R1 = E1 + SHARED1 // I1
WCOLS = HC * P + HC * P + HID
QCHUNKS = 2
LATE = C1 + QCHUNKS
UNIT = 1024
UNITS = LATE * WCOLS // UNIT
HEADS, HD = 16, 16
NS4 = 8
EPS = 1e-5
ATT_EPS = 1e-6

XS = 16.0
WS = 64.0
HS = 4.0
XW = 1.0 / (XS * WS)
P_SCALE = HS / (XS * WS)
HALF = 0.5
ROUTE1_SCALE = 2.5
NEVER = -1e30
TAKEN = -3e38
SENT0, SENT1 = 8 - TOP0, 8 - TOP1
LO_ROW = 32

PQB, PDT, PD = 0, 2, 4
PAR, PAI, PCR, PCI = 6, 22, 38, 54
PR0 = 70
PR1 = PR0 + HC * E0
PCOLS = PR1 + HC * E1

Ffn = namedtuple("Ffn", "phase chunks k0 r0 kind late")


def build(nc, x_in, w0_in, late_in, small_in, bias_in, ow_in, pick_in, ident_in, mask_in, routes, out):
    ctx = ExitStack()
    with ctx:
        def sb(name, shape, dt):
            return ctx.enter_context(nc.sbuf_tensor(name, shape, dt))

        def pb(name, shape, dt):
            return ctx.enter_context(nc.psum_tensor(name, shape, dt))

        def sem(name):
            return ctx.enter_context(nc.semaphore(name))

        x = sb("x", [P, NBLK * TPB, HID], F32)
        w0_hi = sb("w0_hi", [P, C0, WCOLS], F16)
        w0_lo = sb("w0_lo", [P, C0, WCOLS], F16)
        w1_hi = sb("w1_hi", [P, LATE, WCOLS], F16)
        w1_lo = sb("w1_lo", [P, LATE, WCOLS], F16)
        pick = sb("pick", [64, 2 * P], F16)
        xT_hi = sb("xT_hi", [P, HC, NBLK + 1, BLK], F16)
        xT_lo = sb("xT_lo", [P, HC, NBLK + 1, BLK], F16)
        xn = sb("xn", [P, 2, HID], F32)
        wT = sb("wT", [E0, BLK], F32)
        wrow = sb("wrow", [P, 2, BLK], F32)
        bias16 = sb("bias16", [64, 3 * HID], F16)
        diag_hi = sb("diag_hi", [P, NBLK, HC, P], F16)
        diag_lo = sb("diag_lo", [P, NBLK, HC, P], F16)
        o_w = sb("o_w", [P, HC, HID], F32)
        ident = sb("ident", [P, P], F32)
        mask = sb("mask", [P, P], F32)
        GH = P // HD
        kvz = sb("kvz", [P, 2, P + GH], F32)
        zr = sb("zr", [P, TPB, 2, GH], F32)
        small = sb("small", [P, PCOLS], F32)
        rt_hi = sb("rt_hi", [P, PCOLS - PR0], F16)
        rt_lo = sb("rt_lo", [P, PCOLS - PR0], F16)
        bn = sb("bn", [P, TPB, 6], F32)
        mv = sb("mv", [P, TPB, 2], F32)
        mean = sb("mean", [P, 2, TPB], F32)
        ve = sb("ve", [P, 2, TPB], F32)
        mhalf = sb("mhalf", [P, TPB], F32)
        minus1 = sb("minus1", [P, 16], F32)
        rstd = sb("rstd", [P, 2, TPB], F32)
        lb = [sb("lb0", [P, TPB, E0 + SENT0], F32), sb("lb1", [P, TPB, E1 + SENT1], F32)]
        rb = [sb("rb0", [P, TPB, E0 + SENT0], F32), sb("rb1", [P, TPB, E1 + SENT1], F32)]
        m8 = sb("m8", [P, TPB, 8], F32)
        top = [sb("top0", [P, TPB, 8], F32), sb("top1", [P, TPB, 8], F32)]
        ex = sb("ex", [P, TPB, E0], F32)
        wf = [sb("wf0", [P, TPB, E0], F32), sb("wf1", [P, TPB, R1], F32)]
        rsum = sb("rsum", [P, TPB], F32)
        rrec = sb("rrec", [P, TPB], F32)

        WORK = 5896
        work = sb("work", [P, WORK], F32)
        silu = work[:, 0:1024].rearrange("p (a n) -> p a n", a=2)
        qbuf = work[:, 1536:2560].rearrange("p (a n) -> p a n", a=2)
        h_hi = work[:, 2560:3072].bitcast(F16).rearrange("p (a n) -> p a n", a=2)
        h_lo = work[:, 3072:3584].bitcast(F16).rearrange("p (a n) -> p a n", a=2)
        NSTAGE = 2
        STAGE = 3584
        stage = work[:, STAGE:STAGE + NSTAGE * WCOLS].rearrange("p (a n) -> p a n", a=NSTAGE)
        stage_late = work[:, STAGE:STAGE + UNIT]
        S4_AT = STAGE + NSTAGE * WCOLS
        VW = 2 * (P + 1)
        attn = work[:, 0:1024].rearrange("p (g n) -> p g n", g=2)
        k_pos = work[:, 1024:2048].rearrange("p (t n) -> p t n", t=TPB)
        v_sb = work[:, 2048:2048 + TPB * VW].rearrange("p (t n) -> p t n", t=TPB)
        KR = 2048 + TPB * VW
        k_relu = work[:, KR:KR + 512].rearrange("p (s n) -> p s n", s=2)
        QP = KR + 512
        q_pos = work[:, QP:QP + 1024].rearrange("p (m n) -> p m n", m=2)
        q_relu = work[:, QP + 1024:QP + 1536]
        ratio = work[:, QP + 1024:QP + 1536].rearrange("p (s n) -> p s n", s=2)
        bias_raw = work[0:64, S4_AT:S4_AT + 3 * HID]
        assert S4_AT + 3 * HID <= WORK and STAGE + UNIT <= S4_AT

        gate_ps = [pb("gate_ps0", [P, 512], F32), pb("gate_ps1", [P, 512], F32)]
        up_ps = [pb("up_ps0", [P, 512], F32), pb("up_ps1", [P, 512], F32)]
        aux_ps = pb("aux_ps", [P, 512], F32)
        y_ps = [pb("y_ps0", [P, 512], F32), pb("y_ps1", [P, 512], F32)]
        misc = pb("misc", [P, 512], F32)

        def y_tile(t):
            return y_ps[t // 2][:, (t % 2) * HID:(t % 2 + 1) * HID]

        ld_const = sem("ld_const")
        ld_x0 = sem("ld_x0")
        ld_x1 = sem("ld_x1")
        ld_x23 = sem("ld_x23")
        ld_late = sem("ld_late")
        ld_att = sem("ld_att")
        ld_w = [sem(f"ld_w{i}") for i in range(NSTAGE)]
        w_hi_done = sem("w_hi_done")
        w_lo_done = sem("w_lo_done")
        ready = sem("ready")
        par_act = sem("par_act")
        par_pool = sem("par_pool")
        taps_done = sem("taps_done")
        stats = sem("stats")
        rstd_done = sem("rstd_done")
        xn_done = sem("xn_done")
        xT_ps = sem("xT_ps")
        xT_hi_done = sem("xT_hi_done")
        xT_lo_done = sem("xT_lo_done")
        logits_ps = sem("logits_ps")
        route_dve = [sem("route0_dve"), sem("route1_dve")]
        shifted = sem("shifted")
        expd = sem("expd")
        wf_done = sem("wf_done")
        wT_ps = sem("wT_ps")
        wT_done = sem("wT_done")
        wT_out = sem("wT_out")
        ld_wrow = [sem("ld_wrow0"), sem("ld_wrow1")]
        gate_done = sem("gate_done")
        up_done = sem("up_done")
        silu_done = sem("silu_done")
        p_done = sem("p_done")
        q_done = sem("q_done")
        h_hi_done = sem("h_hi_done")
        h_lo_done = sem("h_lo_done")
        down_done = sem("down_done")
        x_done = sem("x_done")
        bias_hi = sem("bias_hi")
        bias_ready = sem("bias_ready")
        kv_ps_done = sem("kv_ps_done")
        k_exp = sem("k_exp")
        k_done = sem("k_done")
        q_ps_done = sem("q_ps_done")
        q_exp = sem("q_exp")
        q_pos_done = sem("q_pos_done")
        sums_ps = sem("sums_ps")
        sums_done = sem("sums_done")
        ratio_ps = sem("ratio_ps")
        den_inv = sem("den_inv")
        ratio_done = sem("ratio_done")
        attn_ps = sem("attn_ps")
        attn_done = sem("attn_done")
        o_ps_done = sem("o_ps_done")
        s4_ps_done = sem("s4_ps_done")
        dve_init = sem("dve_init")
        waited = sem("waited")
        waited_sp = sem("waited_sp")
        stored = sem("stored")

        block = ctx.enter_context(nc.Block())

        FFNS = [Ffn(0, C0, 0, 0, 0, True), Ffn(2, C0, 4 * C0, 4, 0, False),
                Ffn(3, C1, 8 * C0, 8, 1, False), Ffn(5, C1, 8 * C0 + 4 * C1, 12, 1, False)]
        ATT_PHASE, S4_PHASE = 1, 4
        SHAPE = {0: (4, 1, 5), 1: (2, 2, 3)}
        TCH = 4
        for kind, chunks in ((0, C0), (1, C1)):
            ti, tp, ri = SHAPE[kind]
            assert ti * tp == TPB and 1 + ti * TCH + ri + 2 == chunks
        W_HI, W_LO = (w0_hi, w1_hi), (w0_lo, w1_lo)
        late_hi = w1_hi[:, :, :].rearrange("p c n -> p (c n)")
        late_lo = w1_lo[:, :, :].rearrange("p c n -> p (c n)")
        NEXP, NTOP = (E0, E1), (TOP0, TOP1)
        ROWS = (E0, R1)
        RT0 = (0, HC * E0)

        def nxt(b):
            return (b + 1) % NBLK if isinstance(b, int) else (b + 1) & (NBLK - 1)

        def ahead_place(f, b):
            return b + 1 if f.phase == S4_PHASE - 1 else nxt(b)

        def odd(b):
            return b % 2 if isinstance(b, int) else b & 1

        def at(b):
            return b if isinstance(b, int) or b.max_val < NBLK else b & (NBLK - 1)

        def one(ap_index):
            return bass.ds(ap_index, 1)

        def unless_last(eng, b):
            return nullcontext() if isinstance(b, int) else eng.If(b < NBLK - 1)

        def each_block(eng, f, do):
            if f.late:
                do(0, True)
            with eng.Fori(1 if f.late else 0, NBLK) as b:
                do(b, False)

        def route_ahead(eng, f, b, do):
            with unless_last(eng, b):
                do(eng, f, b + 1)
            if f.phase == 2:
                with eng.If(b > NBLK - 2):
                    do(eng, FFNS[2], 0)

        TURN = 2
        LEAD = 2

        S = {}
        s_at = [0]

        def s4_array(name, n=16):
            S[name] = work[:, S4_AT + s_at[0]:S4_AT + s_at[0] + n]
            s_at[0] += n

        for nm in ("dt", "kc0", "kc1", "kc2", "kc3"):
            s4_array(nm, HC)
        for nm in ("are", "a", "ang0", "turn", "ang", "th", "sin", "sh", "em1", "ea", "cm1", "cos", "wre", "wim",
                   "ere", "t1", "t2", "inv", "fre", "fim", "cre", "cim", "nre", "nim", "aren", "omt"):
            s4_array(nm)
        s4_array("sum4", HC * 4)
        s4_array("diag", P)
        assert S4_AT + s_at[0] <= WORK
        S4_Y = (y_ps, up_ps)
        PREP_BANKS = (misc, aux_ps)
        TILE_BANKS = (misc, aux_ps, gate_ps[0], gate_ps[1])
        PAR_A, PAR_T = 2, 10

        def pe_split3(pe, outs, lhs_hi, lhs_lo, rhs_hi, rhs_lo, start, stop, group=True):
            steps = ((lhs_hi, rhs_hi), (lhs_hi, rhs_lo), (lhs_lo, rhs_hi))
            for n, (a, c) in enumerate(steps):
                last = pe.matmul(outs, a, c, start=start and n == 0, stop=stop and n == 2,
                                 skip_group_check=not group)
            return last

        def pe_inner(pe, outs, f, b, c, col):
            hi, lo = W_HI[f.kind], W_LO[f.kind]
            for hc in range(HC):
                a = col + hc * P
                last = pe_split3(pe, outs, hi[:, one(c), a:a + P], lo[:, one(c), a:a + P],
                                 xT_hi[:, hc, one(at(b)), :], xT_lo[:, hc, one(at(b)), :],
                                 hc == 0, hc == HC - 1)
            return last

        def pe_gate_up(pe, f, b, c, par):
            k = f.k0 + b * f.chunks + c
            pe.wait_ge(silu_done, k + 1)
            pe_inner(pe, gate_ps[par][:, :], f, b, c, 0).then_inc(gate_done, 1)
            pe.wait_ge(p_done, k + 1)
            pe_inner(pe, up_ps[par][:, :], f, b, c, HC * P).then_inc(up_done, 1)

        def pe_down(pe, f, b, c, par, first=False, final=False):
            k = f.k0 + b * f.chunks + c
            hi, lo = W_HI[f.kind], W_LO[f.kind]
            w = 2 * HC * P
            if first:
                pe.wait_ge(x_done, 4 * f.phase + b + 4)
            pe.wait_ge(h_lo_done, k + 3)
            for t in range(TPB):
                last = pe_split3(pe, y_tile(t), h_hi[:, par, t * P:(t + 1) * P],
                                 h_lo[:, par, t * P:(t + 1) * P],
                                 hi[:, one(c), w:w + HID], lo[:, one(c), w:w + HID],
                                 first and t % 2 == 0, final, group=False)
            last.then_inc(down_done, 1)

        def pe_transposes(pe, blk, t, slot, routes, bank=misc, banks=1):
            n = TPB * blk + t
            pe.wait_ge(xn_done, n + 1)
            if not (isinstance(n, int) and n < banks):
                pe.wait_ge(xT_lo_done, n + (1 - banks))
            if not (isinstance(routes, int) and routes == 0):
                pe.wait_ge(wT_done, routes)
            for hc in range(HC):
                last = pe.transpose(bank[:, hc * P:(hc + 1) * P], xn[:, slot, hc * P:(hc + 1) * P],
                                    ident[:, :])
            last.then_inc(xT_ps, 1)

        def pe_logits(pe, f, b):
            r, e, o = f.r0 + b, NEXP[f.kind], RT0[f.kind]
            pe.wait_ge(xT_lo_done, TPB * (4 * f.phase + b + 1))
            if not (isinstance(r, int) and r == 0):
                pe.wait_ge(wT_done, r)
            for t in range(TPB):
                for hc in range(HC):
                    last = pe_split3(pe, misc[:, t * e:(t + 1) * e],
                                     xT_hi[:, hc, one(at(b)), t * P:(t + 1) * P],
                                     xT_lo[:, hc, one(at(b)), t * P:(t + 1) * P],
                                     rt_hi[:, o + hc * e:o + (hc + 1) * e],
                                     rt_lo[:, o + hc * e:o + (hc + 1) * e], hc == 0, hc == HC - 1)
            last.then_inc(logits_ps, 1)

        def pe_turn_weights(pe, f, b):
            pe.wait_ge(wf_done, f.r0 + b + 1)
            for t in range(TPB):
                last = pe.transpose(misc[0:ROWS[f.kind], t * P:(t + 1) * P], wf[f.kind][:, t, :], ident[:, :])
            last.then_inc(wT_ps, 1)

        def pe_ffn(pe, f):
            ti, tp, ri = SHAPE[f.kind]
            last_c = f.chunks - 1

            def slot(b, c, par, splitting, turn=False):
                if splitting:
                    pe.wait_ge(w_lo_done, c + 2)
                pe_gate_up(pe, f, b, c + 1, par)
                pe_down(pe, f, b, c - 1, par, first=isinstance(c, int) and c == 1)
                if turn:
                    route_ahead(pe, f, b, pe_turn_weights)

            def do(b, splitting):
                nb = 4 * f.phase + b + 1
                slot(b, 1, 0, splitting)
                with pe.Fori(0, ti) as i:
                    for j in range(TCH):
                        if j == 1:
                            for n in range(tp):
                                pe_transposes(pe, nb, i * tp + n, n, f.r0 + b + 1, PREP_BANKS[n], tp)
                        slot(b, i * TCH + (2 + j), (1 + j) % 2, splitting)
                route_ahead(pe, f, b, pe_logits)
                slot(b, 2 + ti * TCH, 1, splitting)
                for c in range(3 + ti * TCH, last_c):
                    slot(b, c, (c + 1) % 2, splitting, turn=c == last_c - TURN)
                with unless_last(pe, b):
                    pe_gate_up(pe, f, b + 1, 0, 0)
                pe_down(pe, f, b, last_c - 1, 0)
                with unless_last(pe, b):
                    pe_gate_up(pe, f, b + 1, 1, 1)
                pe_down(pe, f, b, last_c, 1, final=True)

            if f.late:
                pe_logits(pe, f, 0)
                pe.wait_ge(w_lo_done, 1)
            pe_gate_up(pe, f, 0, 0, 0)
            if f.late:
                pe_turn_weights(pe, f, 0)
                pe.wait_ge(w_lo_done, 2)
            pe_gate_up(pe, f, 0, 1, 1)
            each_block(pe, f, do)

        ATT = 4 * ATT_PHASE

        def pe_project_kv(pe, b, tiles):
            bank = (gate_ps[0], gate_ps[1])
            if tiles[0] == 0:
                pe.wait_ge(xT_lo_done, TPB * (b + ATT + 1))
            for t in tiles:
                n = TPB * b + t
                if not (isinstance(n, int) and n < 2):
                    pe.wait_ge(k_exp, n - 1)
                pe.matmul(bank[t % 2][:, :], pick[:, 0:P], bias16[:, 0:2 * HID],
                          start=True, stop=False)
                for hc in range(HC):
                    last = pe_split3(pe, bank[t % 2][:, :], xT_hi[:, hc, one(at(b)), t * P:(t + 1) * P],
                                     xT_lo[:, hc, one(at(b)), t * P:(t + 1) * P],
                                     w1_hi[:, C1 + hc, HID:3 * HID], w1_lo[:, C1 + hc, HID:3 * HID],
                                     False, hc == HC - 1)
                last.then_inc(kv_ps_done, 1)
                pe_transposes(pe, b + (ATT + 1), t, t % 2, 4)

        def pe_project_q(pe, b):
            for m in range(HC):
                if m == 1 and not isinstance(b, int):
                    pe.wait_ge(attn_done, TPB * b)
                for hc in range(HC):
                    last = pe_split3(pe, Q_BANKS[m][:, :], w1_hi[:, C1 + hc, m * P:(m + 1) * P],
                                     w1_lo[:, C1 + hc, m * P:(m + 1) * P],
                                     xT_hi[:, hc, one(at(b)), :], xT_lo[:, hc, one(at(b)), :],
                                     hc == 0, hc == HC - 1)
                last.then_inc(q_ps_done, 1)

        Q_BANKS = (up_ps[1], up_ps[0])
        RATIO_BANKS = (up_ps[0], up_ps[1], y_ps[0], y_ps[1])
        TURN_BANKS = (aux_ps, up_ps[0])

        def pe_sums(pe, b):
            pe.wait_ge(k_done, TPB * b + TPB)
            for t in range(TPB):
                for g in range(2):
                    last = pe.matmul(aux_ps[:, g * (P + 1):(g + 1) * (P + 1)],
                                     k_pos[:, t, g * P:(g + 1) * P], v_sb[:, t, g * P:g * P + P + 1],
                                     start=t == 0 and g == 0, stop=t == TPB - 1, skip_group_check=True)
            last.then_inc(sums_ps, 1)

        def pe_ratios(pe, b):
            pe.wait_ge(q_pos_done, 2 * b + 2)
            pe.wait_ge(sums_done, b + 1)
            pe.wait_ge(x_done, b + ATT + 4)
            for t in range(TPB):
                for g in range(2):
                    o = g * (P + GH)
                    last = pe.matmul(RATIO_BANKS[t][:, o:o + P + GH], q_pos[:, g, t * P:(t + 1) * P],
                                     kvz[:, g, :], start=True, stop=True)
                last.then_inc(ratio_ps, 1)

        def pe_turn_ratios(pe, b, t):
            n = TPB * b + t
            pe.wait_ge(ratio_done, n + 1)
            if t >= 2:
                pe.wait_ge(attn_done, n - 1)
            for g in range(2):
                last = pe.transpose(TURN_BANKS[t % 2][:, g * P:(g + 1) * P],
                                    ratio[:, t % 2, g * P:(g + 1) * P], ident[:, :])
            last.then_inc(attn_ps, 1)

        def pe_output(pe, b):
            pe.wait_ge(attn_done, TPB * b + TPB)
            for t in range(TPB):
                pe.matmul(y_tile(t), pick[:, P:2 * P], bias16[:, 2 * HID:3 * HID],
                          start=True, stop=False)
                for g in range(2):
                    last = pe.matmul(y_tile(t), attn[:, g, t * P:(t + 1) * P], o_w[:, g, :],
                                     start=False, stop=g == 1)
            last.then_inc(o_ps_done, 1)

        def pe_attention(pe, f_next):
            pe.wait_ge(bias_ready, 1)
            pe_project_kv(pe, 0, range(TPB))
            pe_project_q(pe, 0)
            with pe.Fori(0, NBLK - 1) as b:
                pe_sums(pe, b)
                pe_project_kv(pe, b + 1, (0, 1))
                pe_ratios(pe, b)
                pe_project_kv(pe, b + 1, (2,))
                pe_turn_ratios(pe, b, 0)
                pe_turn_ratios(pe, b, 1)
                pe_project_kv(pe, b + 1, (3,))
                pe_turn_ratios(pe, b, 2)
                pe_turn_ratios(pe, b, 3)
                pe_project_q(pe, b + 1)
                pe_output(pe, b)
            last = NBLK - 1
            pe_sums(pe, last)
            pe_logits(pe, f_next, 0)
            pe_ratios(pe, last)
            for t in range(TPB):
                pe_turn_ratios(pe, last, t)
            pe_turn_weights(pe, f_next, 0)
            pe_output(pe, last)

        def pe_s4(pe, f_next):
            base = 4 * S4_PHASE
            pe.wait_ge(taps_done, 1)
            for b in range(NBLK):
                for t in range(TPB):
                    pe_transposes(pe, base + b + 1, t, t % 2, 12, TILE_BANKS[t], TPB)
                if b < 2:
                    pe.wait_ge(x_done, base + 4)
                else:
                    pe.wait_ge(x_done, b + base + 3)
                for t in range(TPB):
                    if b == NBLK - 1 and t == TPB // 2:
                        pe_logits(pe, f_next, 0)
                    for hc in range(HC):
                        o = (t % 2) * HID + hc * P
                        for lag in range(b + 1):
                            place = b - lag if b > lag else NBLK
                            last = pe_split3(pe, S4_Y[b % 2][t // 2][:, o:o + P],
                                             xT_hi[:, hc, place, t * P:(t + 1) * P],
                                             xT_lo[:, hc, place, t * P:(t + 1) * P],
                                             diag_hi[:, lag, hc, :], diag_lo[:, lag, hc, :],
                                             lag == 0, lag == b)
                last.then_inc(s4_ps_done, 1)
            pe_turn_weights(pe, f_next, 0)
            pe.wait_ge(x_done, base + NBLK + 4)

        @block.tensor
        def _(pe):
            pe.wait_ge(ld_const, CONSTS)
            pe.wait_ge(ready, 1)
            for t in range(TPB):
                pe_transposes(pe, 0, t, t % 2, 0, TILE_BANKS[t], TPB)
            pe_ffn(pe, FFNS[0])
            pe.wait_ge(w_lo_done, C0 + UNITS)
            pe_attention(pe, FFNS[1])
            pe_ffn(pe, FFNS[1])
            pe_ffn(pe, FFNS[2])
            pe_s4(pe, FFNS[3])
            pe_ffn(pe, FFNS[3])

        def act_silu(a, f, b, c, par):
            k = f.k0 + b * f.chunks + c
            a.wait_ge(gate_done, k + 1)
            a.wait_ge(q_done, k + 1)
            a.activation(silu[:, par, :], gate_ps[par][:, :], ACT.Silu, scale=XW).then_inc(silu_done, 1)

        def act_h_hi(a, f, b, c, par):
            k = f.k0 + b * f.chunks + c
            a.wait_ge(q_done, k + 3)
            a.wait_ge(down_done, k + 1)
            a.activation(h_hi[:, par, :], qbuf[:, par, :], ACT.Copy).then_inc(h_hi_done, 1)

        def act_chunk(a, f, b, c, par):
            act_silu(a, f, b, c, par)
            act_h_hi(a, f, b, c, par)

        def act_xT_hi(a, blk, dst, t, bank=misc):
            n = TPB * blk + t
            a.wait_ge(xT_ps, n + 1)
            a.activation(xT_hi[:, :, one(dst), bass.ds(t * P, P)].rearrange("p h o n -> p h (o n)"),
                         bank[:, 0:HID].rearrange("p (h n) -> p h n", h=HC), ACT.Copy).then_inc(xT_hi_done, 1)

        def act_route_exp(a, f, b):
            a.wait_ge(shifted, f.r0 + b + 1)
            if f.kind == 0:
                a.activation(ex[:, :, :], wf[0][:, :, :], ACT.Exp).then_inc(expd, 1)
            else:
                a.activation(ex[:, :, 0:E1], lb[1][:, :, 0:E1], ACT.Exp, scale=-1.0).then_inc(expd, 1)

        def act_weights_T(a, f, b):
            r, rows = f.r0 + b, ROWS[f.kind]
            a.wait_ge(wT_ps, r + 1)
            if not (isinstance(r, int) and r == 0):
                a.wait_ge(wT_out, 16 * r)
            a.activation(wT[0:rows, :], misc[0:rows, 0:BLK], ACT.Copy).then_inc(wT_done, 1)

        def act_weights_hi(a, n, s):
            a.wait_ge(ld_w[s], (n - s) * (16 // NSTAGE) + 16)
            a.activation(w0_hi[:, one(n), :], stage[:, s, :], ACT.Copy, scale=WS).then_inc(w_hi_done, 1)

        def act_load_weights(a, n, s):
            a.wait_ge(w_lo_done, n - 1)
            a.dma_start(stage[:, s, :], w0_in[one(n)].rearrange("o p n -> (o p) n")).then_inc(ld_w[s], 16)

        def act_load_late(a, n):
            a.wait_ge(w_lo_done, n + C0)
            a.dma_start(stage_late, late_in[one(n)].rearrange("o p n -> (o p) n")).then_inc(ld_late, 16)

        def act_late(a, n):
            a.wait_ge(ld_late, n * 16 + 16)
            a.activation(late_hi[:, bass.ds(n * UNIT, UNIT)], stage_late, ACT.Copy,
                         scale=WS).then_inc(w_hi_done, 1)

        def act_ffn(a, f):
            ti, tp, ri = SHAPE[f.kind]

            def do(b, splitting):
                nb = 4 * f.phase + b + 1

                def slot(c, par, split=True, turn=False, late=None):
                    if splitting and split:
                        act_weights_hi(a, c + LEAD, 1 - par)
                    act_silu(a, f, b, c + 1, par)
                    if splitting and (not isinstance(c, int) or c + 4 < C0):
                        act_load_weights(a, c + 4, 1 - par)
                    if late is not None:
                        act_late(a, late)
                    if turn:
                        route_ahead(a, f, b, act_weights_T)
                    act_h_hi(a, f, b, c + 1, par)

                slot(1, 0)
                if splitting:
                    a.dma_start(x[:, 2 * TPB:, :], x_in[:, 2 * TPB:, :]).then_inc(ld_x23, 16)
                with a.Fori(0, ti) as i:
                    if f.late and not splitting:
                        act_load_late(a, b * ti + i - ti)
                    for j in range(TCH):
                        if j == 2:
                            for n in range(tp):
                                act_xT_hi(a, nb, ahead_place(f, b), i * tp + n, PREP_BANKS[n])
                        is_late = f.late and not splitting and j == TCH - 1
                        slot(i * TCH + (2 + j), (1 + j) % 2, late=b * ti + i - ti if is_late else None)
                route_ahead(a, f, b, act_route_exp)
                slot(2 + ti * TCH, 1)
                for c in range(3 + ti * TCH, f.chunks - 1):
                    slot(c, (c + 1) % 2, c < f.chunks - 2, turn=c == f.chunks - 1 - TURN)
                with unless_last(a, b):
                    act_chunk(a, f, b + 1, 0, 0)
                    act_chunk(a, f, b + 1, 1, 1)

            if f.late:
                act_weights_hi(a, 0, 0)
                act_route_exp(a, f, 0)
                act_weights_hi(a, 1, 1)
                act_load_weights(a, 2, 0)
            act_silu(a, f, 0, 0, 0)
            if f.late:
                act_load_weights(a, 3, 1)
                act_weights_T(a, f, 0)
                act_weights_hi(a, 2, 0)
            act_silu(a, f, 0, 1, 1)
            if f.late:
                act_load_weights(a, 4, 0)
            act_h_hi(a, f, 0, 0, 0)
            act_h_hi(a, f, 0, 1, 1)
            each_block(a, f, do)

        def act_project_kv(a, b, tiles):
            for t in tiles:
                n = TPB * b + t
                a.wait_ge(kv_ps_done, n + 1)
                if not (isinstance(b, int) and b == 0):
                    a.wait_ge(sums_ps, b)
                bank = gate_ps[t % 2]
                a.activation(k_pos[:, t, :], bank[:, 0:HID], ACT.Exp, scale=XW)
                if not (isinstance(n, int) and n < 2):
                    a.wait_ge(k_done, n - 1)
                a.activation(k_relu[:, t % 2, :], bank[:, 0:HID], ACT.Relu, scale=XW)
                a.activation(v_sb[:, t, :].rearrange("p (g n) -> p g n", g=2)[:, :, 0:P],
                             bank[:, HID:2 * HID].rearrange("p (g n) -> p g n", g=2), ACT.Copy,
                             scale=XW).then_inc(k_exp, 1)
                act_xT_hi(a, b + (ATT + 1), nxt(b), t)

        def act_project_q(a, b):
            for m in range(HC):
                bias = small[:, PQB + m:PQB + m + 1]
                a.wait_ge(q_ps_done, 2 * b + m + 1)
                a.activation(q_pos[:, m, :], Q_BANKS[m][:, :], ACT.Exp, scale=XW, bias=bias)
                if not (isinstance(b, int) and b + m == 0):
                    a.wait_ge(q_pos_done, 2 * b + m)
                a.activation(q_relu, Q_BANKS[m][:, :], ACT.Relu, scale=XW, bias=bias).then_inc(q_exp, 1)

        def act_turned(a, b, tiles):
            for t in tiles:
                a.wait_ge(attn_ps, TPB * b + t + 1)
                a.wait_ge(o_ps_done, b + 1)
                a.activation(attn[:, :, t * P:(t + 1) * P],
                             TURN_BANKS[t % 2][:, 0:HID].rearrange("p (g n) -> p g n", g=2),
                             ACT.Copy).then_inc(attn_done, 1)

        def act_attention(a, f_next):
            act_project_kv(a, 0, range(TPB))
            act_project_q(a, 0)
            with a.Fori(0, NBLK - 1) as b:
                act_project_kv(a, b + 1, (0, 1, 2))
                act_turned(a, b, (0, 1))
                act_project_kv(a, b + 1, (3,))
                act_turned(a, b, (2, 3))
                act_project_q(a, b + 1)
            act_route_exp(a, f_next, 0)
            act_turned(a, NBLK - 1, range(TPB))
            act_weights_T(a, f_next, 0)

        def act_s4(a, f_next):
            with a.Fori(0, NBLK) as b:
                for t in range(TPB):
                    act_xT_hi(a, b + (4 * S4_PHASE + 1), nxt(b), t, TILE_BANKS[t])
            act_route_exp(a, f_next, 0)
            act_weights_T(a, f_next, 0)

        @block.scalar
        def _(a):
            for s in (silu_done, h_hi_done):
                a.sem_inc(s, 2)
            a.sem_inc(o_ps_done, 1)
            a.wait_ge(ld_const, CONSTS)
            a.activation(S["dt"], small[:, PDT:PDT + HC], ACT.Exp).then_inc(par_act, 1)
            a.activation(S["are"], small[:, PAR:PAR + 16], ACT.Exp).then_inc(par_act, 1)
            a.wait_ge(par_pool, PAR_A)
            a.activation(S["th"], S["a"], ACT.Tanh, scale=0.5).then_inc(par_act, 1)
            a.wait_ge(par_pool, PAR_T)
            a.activation(S["sin"], S["ang"], ACT.Sin).then_inc(par_act, 1)
            a.activation(S["sh"], S["ang"], ACT.Sin, scale=0.5).then_inc(par_act, 1)
            for t in range(TPB):
                act_xT_hi(a, 0, 0, t, TILE_BANKS[t])
            act_ffn(a, FFNS[0])
            act_attention(a, FFNS[1])
            act_ffn(a, FFNS[1])
            act_ffn(a, FFNS[2])
            act_s4(a, FFNS[3])
            act_ffn(a, FFNS[3])

        class Chain:

            def __init__(self, eng, s, base):
                self.eng, self.s, self.n = eng, s, base

            def step(self, ins):
                ins.then_inc(self.s, 1)
                self.n = self.n + 1

            def then(self, ins):
                self.step(ins)
                self.eng.wait_ge(self.s, self.n)

            def then_alone(self, ins):
                self.then(ins)
                self.eng.sem_inc(waited, 1)

        def dve_stats(v, blk, src):
            ch = Chain(v, stats, blk * 4)
            if not (isinstance(blk, int) and blk == 0):
                v.wait_ge(x_done, blk + 1)
            for t in range(TPB):
                ins = v.bn_stats(bn[:, t, :], x[:, one(src * TPB + t), :])
            ch.then_alone(ins)
            for t in range(TPB):
                ins = v.bn_aggr(mv[:, t, :], bn[:, t, :])
            ch.then(ins)
            ch.step(v.tensor_copy(mean[:, one(odd(blk)), :], mv[:, :, 0].unsqueeze(1)))
            ch.step(v.tensor_scalar(ve[:, one(odd(blk)), :], mv[:, :, 1].unsqueeze(1), EPS, 1.0 / (XS * XS), ALU.add,
                                  ALU.mult))

        def dve_normalise(v, blk, src, t, slot, slots=2):
            n = TPB * blk + t
            v.wait_ge(rstd_done, blk + 1)
            mean_flat = mean[:, :, :].rearrange("p s t -> p (s t)")
            rstd_flat = rstd[:, :, :].rearrange("p s t -> p (s t)")
            if not (isinstance(n, int) and n < slots):
                v.wait_ge(xT_ps, n + (1 - slots))
            v.tensor_scalar(xn[:, slot, :], x[:, one(src * TPB + t), :], mean_flat[:, one(odd(blk) * TPB + t)],
                            rstd_flat[:, one(odd(blk) * TPB + t)], ALU.subtract, ALU.mult).then_inc(xn_done, 1)

        def dve_xT_lo(v, blk, dst, t, bank=misc):
            n = TPB * blk + t
            v.wait_ge(xT_hi_done, n + 1)
            sl = (slice(None), slice(None), one(dst), bass.ds(t * P, P))
            v.tensor_tensor(xT_lo[sl].rearrange("p h o n -> p h (o n)"),
                            bank[:, 0:HID].rearrange("p (h n) -> p h n", h=HC),
                            xT_hi[sl].rearrange("p h o n -> p h (o n)"),
                            ALU.subtract).then_inc(xT_lo_done, 1)

        def dve_first_tiles(v, blk, src):
            for t in range(2):
                dve_normalise(v, blk, src, t, t)

        def dve_tiles(v, blk, src):
            for t in range(TPB):
                dve_xT_lo(v, blk, src, t, TILE_BANKS[t])
                if t + 2 < TPB:
                    dve_normalise(v, blk, src, t + 2, t % 2)

        def route_steps(kind):
            return 7 if kind == 0 else 10

        def dve_route_choose(v, f, b):
            e, k, kind = NEXP[f.kind], NTOP[f.kind], f.kind
            rl = b + (4 if f.phase in (2, 5) else 0)
            ch = Chain(v, route_dve[kind], rl * route_steps(kind))
            v.wait_ge(logits_ps, f.r0 + b + 1)
            ch.then_alone(v.tensor_scalar(lb[kind][:, :, 0:e], misc[:, 0:TPB * e].rearrange("p (t e) -> p t e", t=TPB),
                                    XW, None, ALU.mult))
            for t in range(TPB):
                ins = v.max(m8[:, t, :], lb[kind][:, t, 0:e])
            ch.then(ins)
            if kind == 0:
                v.tensor_tensor(wf[0][:, :, :], lb[0][:, :, 0:e],
                                m8[:, :, 0:1].to_broadcast([P, TPB, e]), ALU.subtract).then_inc(shifted, 1)
            else:
                v.tensor_scalar(m8[:, :, 6:8], m8[:, :, 6:8], 1.0, None, ALU.mult).then_inc(shifted, 1)
            ch.then_alone(v.tensor_copy(top[kind][:, :, 0:k], m8[:, :, 0:k]))
            for t in range(TPB):
                ins = v.match_replace(rb[kind][:, t, :], top[kind][:, t, :], lb[kind][:, t, :], TAKEN)
            ch.step(ins)

        def dve_route_weigh(v, f, b):
            e, kind = NEXP[f.kind], f.kind
            rl = b + (4 if f.phase in (2, 5) else 0)
            ch = Chain(v, route_dve[kind], rl * route_steps(kind) + 4)
            v.wait_ge(route_dve[kind], ch.n)
            v.wait_ge(expd, f.r0 + b + 1)
            prob = ex[:, :, 0:e]
            if kind == 1:
                ch.then(v.tensor_scalar(prob, prob, 1.0, None, ALU.add))
                ch.then(v.reciprocal(prob, prob))
            w = wf[kind][:, :, 0:e]
            ch.then(v.scalar_tensor_tensor(w, rb[kind][:, :, 0:e], TAKEN, prob, ALU.is_equal, ALU.mult))
            ch.then(v.tensor_reduce(rsum[:, :], w, AXX, ALU.add))
            if kind == 1:
                ch.then(v.tensor_scalar(rsum[:, :], rsum[:, :], 1e-20, None, ALU.add))
            ch.then(v.reciprocal(rrec[:, :], rsum[:, :]))
            v.scalar_tensor_tensor(w, w, HALF * (1.0 if kind == 0 else ROUTE1_SCALE),
                                   rrec[:, :].unsqueeze(2).to_broadcast([P, TPB, e]), ALU.mult,
                                   ALU.mult).then_inc(wf_done, 1)

        def dve_h_lo(v, f, b, c, par):
            v.wait_ge(h_hi_done, f.k0 + b * f.chunks + c + 3)
            v.tensor_tensor(h_lo[:, par, :], qbuf[:, par, :], h_hi[:, par, :],
                            ALU.subtract).then_inc(h_lo_done, 1)

        def dve_chunk(v, f, b, c, par, lo=True, split=None, late=None):
            k = f.k0 + b * f.chunks + c
            if split is not None:
                dve_weights_lo(v, split, 1 - par)
            v.wait_ge(silu_done, k + 3)
            v.wait_ge(up_done, k + 1)
            v.scalar_tensor_tensor(silu[:, par, :], up_ps[par][:, :], P_SCALE, silu[:, par, :], ALU.mult,
                                   ALU.mult).then_inc(p_done, 1)
            if late is not None:
                dve_late(v, late)
            v.wait_ge(p_done, k + 3)
            v.wait_ge(ld_wrow[par], 16 * k + (32 - 16 * par))
            v.wait_ge(h_hi_done, k + 1)
            v.tensor_tensor(qbuf[:, par, :], silu[:, par, :], wrow[:, par, :], ALU.mult).then_inc(q_done, 1)
            if lo:
                dve_h_lo(v, f, b, c - 1, 1 - par)

        def dve_add_y(v, phase, b, scale, banks=y_ps):
            for m in range(2):
                xs = x[:, bass.ds(b * TPB + 2 * m, 2), :].rearrange("p t n -> p (t n)")
                ins = v.scalar_tensor_tensor(xs, banks[m][:, :], scale, xs, ALU.mult, ALU.add)
            ins.then_inc(x_done, 1)

        def dve_weights_lo(v, n, s):
            v.wait_ge(w_hi_done, n + 1)
            v.scalar_tensor_tensor(w0_lo[:, one(n), :], stage[:, s, :], WS, w0_hi[:, one(n), :],
                                   ALU.mult, ALU.subtract).then_inc(w_lo_done, 1)

        def dve_late(v, n):
            v.wait_ge(w_hi_done, n + (C0 + 1))
            at_n = bass.ds(n * UNIT, UNIT)
            v.scalar_tensor_tensor(late_lo[:, at_n], stage_late, WS, late_hi[:, at_n],
                                   ALU.mult, ALU.subtract).then_inc(w_lo_done, 1)

        def dve_ffn(v, f):
            ti, tp, ri = SHAPE[f.kind]

            def do(b, splitting):
                nb = 4 * f.phase + b + 1

                def slot(c, par, split=True, late=None):
                    dve_chunk(v, f, b, c + 1, par, split=c + LEAD if splitting and split else None, late=late)

                slot(1, 0)
                with v.Fori(0, ti) as i:
                    for j in range(TCH):
                        if j == 0:
                            for n in range(tp):
                                dve_normalise(v, nb, nxt(b), i * tp + n, n, tp)
                        if j == 2:
                            for n in range(tp):
                                dve_xT_lo(v, nb, ahead_place(f, b), i * tp + n, PREP_BANKS[n])
                        is_late = f.late and not splitting and j == TCH - 1
                        slot(i * TCH + (2 + j), (1 + j) % 2, late=b * ti + i - ti if is_late else None)
                route_ahead(v, f, b, dve_route_choose)
                slot(2 + ti * TCH, 1)
                route_ahead(v, f, b, dve_route_weigh)
                slot(3 + ti * TCH, 0)
                if splitting:
                    v.wait_ge(ld_x23, 16)
                dve_stats(v, nb + 1, nxt(nxt(b)))
                for c in range(4 + ti * TCH, f.chunks - 1):
                    slot(c, (c + 1) % 2, c < f.chunks - 2)
                with unless_last(v, b):
                    dve_chunk(v, f, b + 1, 0, 0)
                    dve_chunk(v, f, b + 1, 1, 1)
                if not isinstance(b, int):
                    with v.If(b > NBLK - 2):
                        dve_h_lo(v, f, b, f.chunks - 1, 1)
                        if f.phase == 0:
                            dve_attention_ahead(v)
                        if f.phase in (0, 3):
                            dve_first_tiles(v, 4 * f.phase + 5, 1)
                v.wait_ge(down_done, f.k0 + b * f.chunks + (f.chunks + 2))
                dve_add_y(v, f.phase, b, 1.0 / (HS * WS))

            if f.late:
                dve_weights_lo(v, 0, 0)
                dve_route_choose(v, f, 0)
                dve_weights_lo(v, 1, 1)
                dve_route_weigh(v, f, 0)
                dve_weights_lo(v, 2, 0)
                v.wait_ge(ld_x1, 16)
                dve_stats(v, 1, 1)
            dve_chunk(v, f, 0, 0, 0, lo=False)
            dve_chunk(v, f, 0, 1, 1)
            each_block(v, f, do)

        def dve_project_kv(v, b, tiles):
            blk = b + (ATT + 1)
            for t in tiles:
                n = TPB * b + t
                v.wait_ge(k_exp, n + 1)
                v.scalar_tensor_tensor(k_pos[:, t, :], k_pos[:, t, :], 1.0, k_relu[:, t % 2, :],
                                       ALU.min, ALU.add).then_inc(k_done, 1)
                dve_xT_lo(v, blk, nxt(b), t)
                if t + 2 < TPB:
                    dve_normalise(v, blk, nxt(b), t + 2, t % 2)
            if tiles[-1] == TPB - 1:
                dve_stats(v, blk + 1, nxt(nxt(b)))

        def dve_project_q(v, b):
            for m in range(HC):
                v.wait_ge(q_exp, 2 * b + m + 1)
                v.scalar_tensor_tensor(q_pos[:, m, :], q_pos[:, m, :], 1.0, q_relu, ALU.min,
                                       ALU.add).then_inc(q_pos_done, 1)

        def dve_sums(v, b):
            v.wait_ge(sums_ps, b + 1)
            w = P + 1
            heads = mask[:, :].rearrange("p (h d) -> p h d", d=HD)[:, :, 0]
            v.tensor_tensor(kvz[:, 0, 0:P], aux_ps[:, 0:P], mask[:, :], ALU.mult)
            v.tensor_scalar(kvz[:, 0, P:], heads, aux_ps[:, P:w], None, ALU.mult)
            v.tensor_tensor(kvz[:, 1, 0:P], aux_ps[:, w + 1:2 * w], mask[:, :], ALU.mult)
            v.tensor_scalar(kvz[:, 1, P:], heads, aux_ps[:, w:w + 1], None,
                            ALU.mult).then_inc(sums_done, 1)

        def dve_ratios(v, b):
            for t in range(TPB):
                n = TPB * b + t
                ps = RATIO_BANKS[t][:, 0:2 * (P + GH)].rearrange("p (g n) -> p g n", g=2)
                v.wait_ge(ratio_ps, n + 1)
                v.tensor_scalar(zr[:, t, :, :], ps[:, :, P:], ATT_EPS, None, ALU.add).then_inc(den_inv, 1)
                v.wait_ge(den_inv, 2 * n + 1)
                v.reciprocal(zr[:, t, :, :], zr[:, t, :, :]).then_inc(den_inv, 1)
                v.wait_ge(den_inv, 2 * n + 2)
                if t >= 2:
                    v.wait_ge(attn_ps, n - 1)
                for g in range(2):
                    ins = v.tensor_tensor(
                        ratio[:, t % 2, g * P:(g + 1) * P].rearrange("p (h d) -> p h d", d=HD),
                        ps[:, g, 0:P].rearrange("p (h d) -> p h d", d=HD),
                        zr[:, t, g, :].unsqueeze(2).to_broadcast([P, GH, HD]), ALU.mult)
                ins.then_inc(ratio_done, 1)

        def dve_output(v, b):
            v.wait_ge(o_ps_done, b + 2)
            dve_add_y(v, ATT_PHASE, b, 1.0)

        def dve_attention_ahead(v):
            v.wait_ge(ld_att, 64)
            v.tensor_copy(bias16[:, :], bias_raw).then_inc(bias_hi, 1)
            v.wait_ge(bias_hi, 1)
            v.tensor_tensor(bias16[LO_ROW:2 * LO_ROW, :], bias_raw[LO_ROW:2 * LO_ROW, :],
                            bias16[LO_ROW:2 * LO_ROW, :], ALU.subtract).then_inc(bias_ready, 1)

        def dve_attention(v, f_next):
            for t in range(TPB):
                v.memset(v_sb[:, t, P:P + 1], 1.0)
            dve_project_kv(v, 0, range(TPB))
            dve_project_q(v, 0)
            with v.Fori(0, NBLK - 1) as b:
                dve_first_tiles(v, b + (ATT + 2), nxt(b + 1))
                dve_sums(v, b)
                dve_project_kv(v, b + 1, (0, 1))
                dve_ratios(v, b)
                dve_project_kv(v, b + 1, (2, 3))
                dve_project_q(v, b + 1)
                dve_output(v, b)
            last = NBLK - 1
            dve_sums(v, last)
            dve_route_choose(v, f_next, 0)
            dve_ratios(v, last)
            dve_route_weigh(v, f_next, 0)
            dve_output(v, last)

        def dve_s4(v, f_next):
            base = 4 * S4_PHASE
            for b in range(NBLK):
                dve_tiles(v, base + b + 1, (b + 1) % NBLK)
                if b < NBLK - 1:
                    dve_stats(v, base + b + 2, (b + 2) % NBLK)
                    dve_first_tiles(v, base + b + 2, (b + 2) % NBLK)
                else:
                    dve_route_choose(v, f_next, 0)
                    dve_route_weigh(v, f_next, 0)
                v.wait_ge(s4_ps_done, b + 1)
                dve_add_y(v, S4_PHASE, b, XW, S4_Y[b % 2])
            dve_stats(v, base + NBLK + 1, 1)

        @block.vector
        def _(v):
            for s in (p_done, q_done, h_lo_done):
                v.sem_inc(s, 2)
            v.sem_inc(down_done, 2)
            ch = Chain(v, dve_init, 0)
            ch.step(v.memset(mhalf[:, :], -0.5))
            for s, (e, k) in enumerate(((E0, TOP0), (E1, TOP1))):
                ch.step(v.memset(lb[s][:, :, e:e + 8 - k], NEVER))
                ch.step(v.memset(top[s][:, :, k:8], NEVER))
            ch.step(v.memset(wf[1][:, :, E1:R1], HALF))
            v.wait_ge(ld_const, CONSTS)
            ch.then(v.tensor_scalar(rt_hi[:, :], small[:, PR0:PCOLS], WS, None, ALU.mult))
            ch.then(v.scalar_tensor_tensor(rt_lo[:, :], small[:, PR0:PCOLS], WS, rt_hi[:, :], ALU.mult,
                                           ALU.subtract))
            v.sem_inc(ready, 1)
            v.wait_ge(ld_x0, 16)
            dve_stats(v, 0, 0)
            v.sem_inc(x_done, NBLK)
            dve_first_tiles(v, 0, 0)
            dve_tiles(v, 0, 0)
            dve_ffn(v, FFNS[0])
            dve_attention(v, FFNS[1])
            dve_ffn(v, FFNS[1])
            dve_ffn(v, FFNS[2])
            dve_s4(v, FFNS[3])
            dve_ffn(v, FFNS[3])

        def pool_s4_angles(v):
            ch = Chain(v, par_pool, 0)
            tt = v.tensor_tensor
            v.wait_ge(par_act, 2)
            dtb = S["dt"].unsqueeze(2).to_broadcast([P, HC, NS4])
            ch.then(v.tensor_scalar(S["aren"], S["are"], -1.0, None, ALU.mult))
            ch.then(tt(per_state(S["a"]), per_state(S["aren"]), dtb, ALU.mult))
            assert ch.n == PAR_A
            ch.then(tt(per_state(S["ang0"]), per_state(small[:, PAI:PAI + 16]), dtb, ALU.mult))
            magic = 12582912.0
            ch.then(v.tensor_scalar(S["turn"], S["ang0"], 1.0 / (2 * np.pi), magic, ALU.mult, ALU.add))
            ch.then(v.tensor_scalar(S["turn"], S["turn"], magic, None, ALU.subtract))
            c1 = 6.28125
            c2 = 2 * np.pi - c1
            for part in (c1, c2):
                ch.then(v.tensor_scalar(S["t1"], S["turn"], part, None, ALU.mult))
                ch.then(tt(S["ang0"], S["ang0"], S["t1"], ALU.subtract))
            ch.then(v.tensor_scalar(S["ang"], S["ang0"], 3.1415925, -3.1415925, ALU.min, ALU.max))
            assert ch.n == PAR_T

        def per_state(ap):
            return ap.rearrange("p (h n) -> p h n", h=HC)

        def pool_s4_taps(v):
            ch = Chain(v, par_pool, PAR_T)
            tt = v.tensor_tensor
            ai = small[:, PAI:PAI + 16]

            def inverse(ap):
                ch.then(tt(ap, ap, minus1[:, :], ALU.pow))

            v.wait_ge(par_act, 5)
            ch.then(v.tensor_scalar(S["omt"], S["th"], -1.0, 1.0, ALU.mult, ALU.add))
            inverse(S["omt"])
            ch.then(v.tensor_scalar(S["t1"], S["th"], 2.0, None, ALU.mult))
            ch.then(tt(S["em1"], S["t1"], S["omt"], ALU.mult))
            ch.then(v.tensor_scalar(S["ea"], S["em1"], 1.0, None, ALU.add))
            ch.then(v.tensor_scalar(S["t1"], S["sh"], -2.0, None, ALU.mult))
            ch.then(tt(S["cm1"], S["t1"], S["sh"], ALU.mult))
            ch.then(v.tensor_scalar(S["cos"], S["cm1"], 1.0, None, ALU.add))
            ch.then(tt(S["wre"], S["ea"], S["cos"], ALU.mult))
            ch.then(tt(S["wim"], S["ea"], S["sin"], ALU.mult))
            ch.then(tt(S["t1"], S["em1"], S["cos"], ALU.mult))
            ch.then(tt(S["ere"], S["t1"], S["cm1"], ALU.add))

            def product(re, im, are, aim, bre, bim):
                ch.then(tt(S["t1"], aim, bim, ALU.mult))
                ch.then(tt(S["t2"], are, bre, ALU.mult))
                ch.then(tt(re, S["t2"], S["t1"], ALU.subtract))
                ch.then(tt(S["t1"], are, bim, ALU.mult))
                ch.then(tt(S["t2"], aim, bre, ALU.mult))
                ch.then(tt(im, S["t2"], S["t1"], ALU.add))

            ch.then(tt(S["t1"], S["aren"], S["aren"], ALU.mult))
            ch.then(tt(S["t2"], ai, ai, ALU.mult))
            ch.then(tt(S["inv"], S["t1"], S["t2"], ALU.add))
            inverse(S["inv"])
            ch.then(v.tensor_scalar(S["nim"], ai, -1.0, None, ALU.mult))
            product(S["fre"], S["fim"], S["ere"], S["wim"], S["aren"], S["nim"])
            ch.then(tt(S["fre"], S["fre"], S["inv"], ALU.mult))
            ch.then(tt(S["fim"], S["fim"], S["inv"], ALU.mult))
            product(S["cre"], S["cim"], small[:, PCR:PCR + 16], small[:, PCI:PCI + 16], S["fre"], S["fim"])
            for lag in range(NBLK):
                kc = S[f"kc{lag}"]
                terms, halves = per_state(S["cre"]), S["sum4"].rearrange("p (h n) -> p h n", h=HC)
                ch.then(tt(halves[:, :, 0:4], terms[:, :, 0:4], terms[:, :, 4:8], ALU.add))
                ch.then(tt(halves[:, :, 0:2], halves[:, :, 0:2], halves[:, :, 2:4], ALU.add))
                ch.then(tt(kc.unsqueeze(2), halves[:, :, 0:1], halves[:, :, 1:2], ALU.add))
                ch.then(v.tensor_scalar(kc, kc, 2.0 * WS, None, ALU.mult))
                if lag == 0:
                    ch.then(v.tensor_scalar(S["t1"][:, 0:HC], small[:, PD:PD + HC], WS, None, ALU.mult))
                    ch.then(tt(kc, kc, S["t1"][:, 0:HC], ALU.add))
                for hc in range(HC):
                    ch.then(v.tensor_scalar(S["diag"], ident[:, :], kc[:, hc:hc + 1], None, ALU.mult))
                    ch.then(v.tensor_copy(diag_hi[:, lag, hc, :], S["diag"]))
                    ch.then(tt(diag_lo[:, lag, hc, :], S["diag"], diag_hi[:, lag, hc, :], ALU.subtract))
                if lag < NBLK - 1:
                    product(S["nre"], S["nim"], S["cre"], S["cim"], S["wre"], S["wim"])
                    ch.then(v.tensor_copy(S["cre"], S["nre"]))
                    ch.then(v.tensor_copy(S["cim"], S["nim"]))
            v.sem_inc(taps_done, 1)

        @block.gpsimd
        def _(pool):
            def rsqrt(blk):
                pool.wait_ge(stats, 4 * blk + 4)
                pool.tensor_tensor(rstd[:, one(odd(blk)), :], ve[:, one(odd(blk)), :], mhalf[:, :].unsqueeze(1), ALU.pow).then_inc(rstd_done, 1)

            pool.memset(minus1[:, :], -1.0)
            pool.wait_ge(ld_const, CONSTS)
            pool_s4_angles(pool)
            pool.wait_ge(dve_init, 6)
            rsqrt(0)
            rsqrt(1)
            pool_s4_taps(pool)
            with pool.Fori(2, NBLK * 6 + 2) as i:
                rsqrt(i)

        PERIOD, EPERIOD = 6, 8
        assert PERIOD * P == EPERIOD * I0 and C0 % PERIOD == 0

        def pieces_of(c, inner):
            first = c * P // inner
            rows = min(P, (first + 1) * inner - c * P)
            return [(first, rows), (first + 1, P - rows)] if rows < P else [(first, P // 2)] * 2

        @block.sync
        def _(sp):
            sp.dma_start(small[:, :], small_in).then_inc(ld_const, 16)
            sp.dma_start(x[:, 0:TPB, :], x_in[:, 0:TPB, :]).then_inc(ld_x0, 16)
            sp.dma_start(ident[:, :], ident_in).then_inc(ld_const, 16)
            for s in range(NSTAGE):
                sp.dma_start(stage[:, s, :], w0_in[s]).then_inc(ld_w[s], 16)
            sp.dma_start(x[:, TPB:2 * TPB, :], x_in[:, TPB:2 * TPB, :]).then_inc(ld_x1, 16)
            sp.dma_start(o_w[:, :, :], ow_in).then_inc(ld_att, 16)
            sp.dma_start(mask[:, :], mask_in).then_inc(ld_att, 16)
            sp.dma_start(pick[:, :], pick_in).then_inc(ld_att, 16)

            def wait_alone(s, value):
                sp.wait_ge(s, value)
                sp.sem_inc(waited_sp, 1)

            def spread(f, b, c, par, pieces):
                k = f.k0 + b * f.chunks + c
                wait_alone(q_done, k + 1)
                first = 0
                for e, count in pieces:
                    row = routes[one(odd(b)), one(e), :].rearrange("o p n -> (o p) n")
                    sp.dma_start(wrow[first:first + count, par, :], row.to_broadcast([count, BLK])).then_inc(
                        ld_wrow[par], 16)
                    first += count

            for f in FFNS:
                with sp.Fori(0, NBLK) as b:
                    r = f.r0 + b
                    wait_alone(wT_done, r + 1)
                    sp.dma_start(routes[one(odd(b)), 0:ROWS[f.kind], :].rearrange("o p n -> (o p) n"),
                                 wT[0:ROWS[f.kind], :]).then_inc(wT_out, 16)
                    wait_alone(wT_out, 16 * r + 16)
                    if f.kind == 0:
                        with sp.Fori(0, C0 // PERIOD) as i:
                            for c in range(PERIOD):
                                pieces = [(i * EPERIOD + e, n) for e, n in pieces_of(c, I0)]
                                spread(f, b, i * PERIOD + c, c % 2, pieces)
                    else:
                        for c in range(C1):
                            spread(f, b, c, c % 2, [(min(e, R1 - 1), n) for e, n in pieces_of(c, I1)])
                if f.late:
                    sp.wait_ge(taps_done, 1)
                    sp.dma_start(bias_raw, bias_in.to_broadcast([64, 3 * HID])).then_inc(ld_att, 16)
            base = 4 * 5 + 4
            with sp.Fori(0, NBLK) as b:
                sp.wait_ge(x_done, b + base + 1)
                sp.dma_start(out[:, bass.ds(b * TPB, TPB), :], x[:, bass.ds(b * TPB, TPB), :]).then_inc(
                    stored, 16)
            sp.wait_ge(stored, 16 * NBLK)


CONSTS = 32


def kernel(**inputs):
    import numpy as _np
    import concourse.bacc as _bacc
    from concourse import mybir as _mybir
    from concourse.bass_utils import run_bass_kernel_spmd as _run

    f32 = _np.float32
    a = {k: _np.asarray(v) for k, v in inputs.items()}

    def chunks_of_rows(w, n):
        pad = _np.zeros((n * P - w.shape[0], w.shape[1]), w.dtype)
        w = _np.concatenate([w, pad], 0).reshape(n, P, HC, P)
        return w.transpose(0, 3, 2, 1).reshape(n, P, HC * P)

    def chunks_of_down(w, n):
        pad = _np.zeros((n * P - w.shape[0], w.shape[1]), w.dtype)
        return _np.concatenate([w, pad], 0).reshape(n, P, HID)

    def rows(w):
        return w.reshape(-1, w.shape[-1])

    w0 = _np.concatenate([
        chunks_of_rows(rows(a["L0_ffn_gate_w"]), C0), chunks_of_rows(rows(a["L0_ffn_up_w"]), C0),
        chunks_of_down(rows(a["L0_ffn_down_w"].transpose(0, 2, 1)), C0)], 2)
    gate1 = _np.concatenate([rows(a["L1_ffn_exp_wg"]), a["L1_ffn_shared_wg"]], 0)
    up1 = _np.concatenate([rows(a["L1_ffn_exp_wu"]), a["L1_ffn_shared_wu"]], 0)
    down1 = _np.concatenate([rows(a["L1_ffn_exp_wd"].transpose(0, 2, 1)), a["L1_ffn_shared_wd"].T], 0)
    w1 = _np.concatenate([chunks_of_rows(gate1, C1), chunks_of_rows(up1, C1), chunks_of_down(down1, C1)], 2)
    qkv = _np.concatenate([a["L0_attn_q_w"].T, a["L0_attn_k_w"].T, a["L0_attn_v_w"].T], 1).reshape(HC, P, 3 * HID)
    late = _np.concatenate([w1, qkv], 0).transpose(1, 0, 2).reshape(P, UNITS, UNIT).transpose(1, 0, 2)

    def halves(v):
        v = v.reshape(HC, P, -1)
        return v.transpose(1, 0, 2).reshape(P, -1)

    small = _np.concatenate([
        halves(a["L0_attn_q_b"]), halves(a["L1_attn_log_dt"]), halves(a["L1_attn_D_param"]),
        halves(a["L1_attn_A_real_log"]), halves(a["L1_attn_A_imag"]), halves(a["L1_attn_C_re"]),
        halves(a["L1_attn_C_im"]), halves(a["L0_ffn_router_w"].T), halves(a["L1_ffn_gate_w"].T)], 1)
    bias = _np.concatenate([a["L0_attn_k_b"], a["L0_attn_v_b"], a["L0_attn_o_b"]]).reshape(1, 3 * HID)
    ow = a["L0_attn_o_w"].T.reshape(HC, P, HID).transpose(1, 0, 2)
    ident = _np.eye(P, dtype=f32)
    mask = _np.kron(_np.eye(P // HD), _np.ones((HD, HD))).astype(f32)
    pick = _np.zeros((64, 2 * P), _np.float16)
    for n, scale in enumerate((XS * WS, 1.0)):
        pick[0, n * P:(n + 1) * P] = pick[LO_ROW, n * P:(n + 1) * P] = scale
    xin = a["L0_attn_hidden_states"].reshape(NBLK * TPB, P, HID).transpose(1, 0, 2)

    given = dict(x=xin, w0=w0, late=late, small=small, bias=bias, ow=ow, pick=pick, ident=ident, mask=mask)
    nc = _bacc.Bacc("TRN2", target_bir_lowering=False, num_devices=1)
    arrays = {f"{n}_dram": _np.ascontiguousarray(v) for n, v in given.items()}
    d = {n: nc.dram_tensor(f"{n}_dram", arrays[f"{n}_dram"].shape,
                           _mybir.dt.from_np(arrays[f"{n}_dram"].dtype), kind="ExternalInput").ap()
         for n in given}
    routes = nc.dram_tensor("routes_dram", (2, E0, BLK), F32, kind="Internal").ap()
    out = nc.dram_tensor("out_0_dram", (P, NBLK * TPB, HID), F32, kind="ExternalOutput").ap()
    build(nc, d["x"], d["w0"], d["late"], d["small"], d["bias"], d["ow"], d["pick"], d["ident"],
          d["mask"], routes, out)
    r = _run(nc, [arrays], core_ids=[0])
    return r.results[0]["out_0_dram"].transpose(1, 0, 2).reshape(NBLK, BLK, HID)
```
